# Optimizing a Trainium2 kernel written in Bass

```python
import numpy as np
import jax
import jax.numpy as jnp

def _softmax(x, axis=-1):
    return jax.nn.softmax(x, axis=axis)

def _gelu(x):
    return jax.nn.gelu(x, approximate=True)

def _silu(x):
    return jax.nn.silu(x)

def _sigmoid(x):
    return jax.nn.sigmoid(x)

def _layernorm(x, axis=-1, eps=1e-05):
    m = jnp.mean(x, axis=axis, keepdims=True)
    v = jnp.var(x, axis=axis, keepdims=True)
    return (x - m) / jnp.sqrt(v + eps)

def _scatter_add(tgt, idx, src, axis=0):
    return tgt.at[idx].add(src)

def _segment_sum(src, seg, n):
    return jax.ops.segment_sum(src, seg, n)
kernel_name = 'mk_sandwich_d2_jaxref_r8_2b9d07'

def setup_inputs(seed: int=0):
    np.random.seed(seed)
    _w = jnp.asarray

    def _L0_attn_setup():
        import jax, jax.numpy as jnp
        import numpy as np
        ALPHA = 0.99
        EMBED_DIM = 128
        SEQ_LEN = 256
        BATCH = 4
        key = jax.random.key(seed)
        k1, k2, k3 = jax.random.split(key, 3)
        x = jax.random.normal(k1, (BATCH, SEQ_LEN, EMBED_DIM), dtype=jnp.float32)
        scale = 1.0 / np.sqrt(EMBED_DIM)
        W_qkv = jax.random.uniform(k2, (3 * EMBED_DIM, EMBED_DIM), dtype=jnp.float32, minval=-scale, maxval=scale)
        b_qkv = jax.random.uniform(k3, (3 * EMBED_DIM,), dtype=jnp.float32, minval=-scale, maxval=scale)
        return {'x': x, 'W_qkv': W_qkv, 'b_qkv': b_qkv}
    _L0_attn_in = _L0_attn_setup()

    def _L0_ffn_setup():
        import jax, jax.numpy as jnp
        import numpy as np
        TOP_K = 2

        def _mlp(x, w_fc, w_proj):
            return jnp.square(jax.nn.relu(x @ w_fc.T)) @ w_proj.T
        key = jax.random.key(seed)
        ks = jax.random.split(key, 6)
        B, S, D, E = (4, 256, 128, 8)
        d_ff = 4 * D
        x = jax.random.normal(ks[0], (B, S, D), dtype=jnp.float32)
        router_w = jax.random.normal(ks[1], (E, D), dtype=jnp.float32) * 0.02
        w_fc = jax.random.normal(ks[2], (E, d_ff, D), dtype=jnp.float32) * 0.02
        w_proj = jax.random.normal(ks[3], (E, D, d_ff), dtype=jnp.float32) * 0.02
        shared_fc = jax.random.normal(ks[4], (d_ff, D), dtype=jnp.float32) * 0.02
        shared_proj = jax.random.normal(ks[5], (D, d_ff), dtype=jnp.float32) * 0.02
        return {'x': x, 'router_w': router_w, 'w_fc': w_fc, 'w_proj': w_proj, 'shared_fc': shared_fc, 'shared_proj': shared_proj}
    _L0_ffn_in = _L0_ffn_setup()

    def _L1_attn_setup():
        import jax, jax.numpy as jnp
        import numpy as np
        B, T, D = (4, 512, 128)
        EPS = 1e-06
        key = jax.random.key(seed)
        ks = jax.random.split(key, 9)
        s = 0.02
        f32 = jnp.float32
        return {'x_seq': jax.random.normal(ks[0], (B, T, D), f32), 'W_q': jax.random.normal(ks[1], (D, D), f32) * s, 'b_q': jax.random.normal(ks[2], (D,), f32) * s, 'W_k': jax.random.normal(ks[3], (D, D), f32) * s, 'b_k': jax.random.normal(ks[4], (D,), f32) * s, 'W_v': jax.random.normal(ks[5], (D, D), f32) * s, 'b_v': jax.random.normal(ks[6], (D,), f32) * s, 'W_a': jax.random.normal(ks[7], (D, D), f32) * s, 'b_a': jax.random.normal(ks[8], (D,), f32) * s}
    _L1_attn_in = _L1_attn_setup()

    def _L1_ffn_setup():
        import jax, jax.numpy as jnp
        import numpy as np
        DIM = 128
        DEPTH = 2
        HEADS = 8
        DIM_HEAD = 64
        WINDOW = 64
        INNER = HEADS * DIM_HEAD
        HID = int(DIM * 4 * 2 / 3)
        B, N = (2, 1024)
        QK_SCALE = 8.0

        def shift_token(t):
            t1, t2 = jnp.split(t, 2, axis=-1)
            t2 = jnp.pad(t2, ((0, 0), (1, 0), (0, 0)))[:, :-1]
            return jnp.concatenate([t1, t2], axis=-1)

        def l2norm(t):
            return t / jnp.clip(jnp.linalg.norm(t, axis=-1, keepdims=True), 1e-12)

        def rotate_half(x):
            x1, x2 = jnp.split(x, 2, axis=-1)
            return jnp.concatenate([-x2, x1], axis=-1)

        def rotary_xpos(q, k):
            n = q.shape[-2]
            half_idx = jnp.arange(0, DIM_HEAD, 2, dtype=jnp.float32)
            inv_freq = 1.0 / 10000.0 ** (half_idx / DIM_HEAD)
            t = jnp.arange(n, dtype=jnp.float32)
            freqs = t[:, None] * inv_freq[None, :]
            freqs = jnp.concatenate([freqs, freqs], axis=-1)
            base = (half_idx + 0.4 * DIM_HEAD) / (1.4 * DIM_HEAD)
            power = (t - n // 2) / float(WINDOW // 2)
            scale = base[None, :] ** power[:, None]
            scale = jnp.concatenate([scale, scale], axis=-1)
            cos, sin = (jnp.cos(freqs), jnp.sin(freqs))
            q = q * cos * scale + rotate_half(q) * sin * scale
            k = k * cos / scale + rotate_half(k) * sin / scale
            return (q, k)

        def local_attention(q, k, v):
            b, h, n, d = q.shape
            w = n // WINDOW
            bq = q.reshape(b, h, w, WINDOW, d) * QK_SCALE
            bk = k.reshape(b, h, w, WINDOW, d)
            bv = v.reshape(b, h, w, WINDOW, d)

            def look_around(t):
                p = jnp.pad(t, ((0, 0), (0, 0), (1, 0), (0, 0), (0, 0)))
                return jnp.concatenate([p[:, :, :w], p[:, :, 1:]], axis=3)
            bk, bv = (look_around(bk), look_around(bv))
            bt = jnp.arange(n).reshape(w, WINDOW)
            btp = jnp.pad(bt, ((1, 0), (0, 0)), constant_values=-1)
            btk = jnp.concatenate([btp[:w], btp[1:]], axis=1)
            sim = jnp.einsum('bhwid,bhwjd->bhwij', bq, bk)
            i = bt[:, :, None]
            j = btk[:, None, :]
            mask = (i < j) | (i > j + WINDOW) | (j == -1)
            sim = jnp.where(mask, -jnp.finfo(sim.dtype).max, sim)
            attn = jax.nn.softmax(sim, axis=-1)
            out = jnp.einsum('bhwij,bhwjd->bhwid', attn, bv)
            return out.reshape(b, h, n, d)

        def _layer(x, wqkv, qs, ksc, wo, lg, lb, w1, b1, w2, b2):
            b, n, _ = x.shape
            h = shift_token(x)
            qkv = h @ wqkv
            q, k, v = jnp.split(qkv, 3, axis=-1)
            to_heads = lambda t: t.reshape(b, n, HEADS, DIM_HEAD).transpose(0, 2, 1, 3)
            q, k, v = (to_heads(q), to_heads(k), to_heads(v))
            q = l2norm(q) * qs
            k = l2norm(k) * ksc
            q, k = rotary_xpos(q, k)
            o = local_attention(q, k, v)
            o = o.transpose(0, 2, 1, 3).reshape(b, n, INNER)
            x = x + o @ wo
            h = shift_token(x)
            mu = h.mean(-1, keepdims=True)
            var = h.var(-1, keepdims=True)
            h = (h - mu) / jnp.sqrt(var + 1e-05) * lg + lb
            h = h @ w1 + b1
            a, g = jnp.split(h, 2, axis=-1)
            h = a * jax.nn.gelu(g, approximate=False)
            x = x + h @ w2 + b2
            return x
        key = jax.random.key(seed)
        ks = jax.random.split(key, 6)
        return {'x': jax.random.normal(ks[0], (B, N, DIM), jnp.float32), 'wqkv': jax.random.normal(ks[1], (DEPTH, DIM, 3 * INNER), jnp.float32) * 0.02, 'q_scale': jnp.ones((DEPTH, DIM_HEAD), jnp.float32), 'k_scale': jnp.ones((DEPTH, DIM_HEAD), jnp.float32), 'wo': jax.random.normal(ks[2], (DEPTH, INNER, DIM), jnp.float32) * 0.02, 'ln_g': jnp.ones((DEPTH, DIM), jnp.float32), 'ln_b': jnp.zeros((DEPTH, DIM), jnp.float32), 'w1': jax.random.normal(ks[3], (DEPTH, DIM, 2 * HID), jnp.float32) * 0.02, 'b1': jnp.zeros((DEPTH, 2 * HID), jnp.float32), 'w2': jax.random.normal(ks[4], (DEPTH, HID, DIM), jnp.float32) * 0.02, 'b2': jnp.zeros((DEPTH, DIM), jnp.float32)}
    _L1_ffn_in = _L1_ffn_setup()
    _d = {'L0_attn_x': _L0_attn_in['x'], 'L0_attn_W_qkv': _L0_attn_in['W_qkv'], 'L0_attn_b_qkv': _L0_attn_in['b_qkv'], 'L0_ffn_router_w': _L0_ffn_in['router_w'], 'L0_ffn_w_fc': _L0_ffn_in['w_fc'], 'L0_ffn_w_proj': _L0_ffn_in['w_proj'], 'L0_ffn_shared_fc': _L0_ffn_in['shared_fc'], 'L0_ffn_shared_proj': _L0_ffn_in['shared_proj'], 'L1_attn_W_q': _L1_attn_in['W_q'], 'L1_attn_b_q': _L1_attn_in['b_q'], 'L1_attn_W_k': _L1_attn_in['W_k'], 'L1_attn_b_k': _L1_attn_in['b_k'], 'L1_attn_W_v': _L1_attn_in['W_v'], 'L1_attn_b_v': _L1_attn_in['b_v'], 'L1_attn_W_a': _L1_attn_in['W_a'], 'L1_attn_b_a': _L1_attn_in['b_a'], 'L1_ffn_wqkv': _L1_ffn_in['wqkv'], 'L1_ffn_q_scale': _L1_ffn_in['q_scale'], 'L1_ffn_k_scale': _L1_ffn_in['k_scale'], 'L1_ffn_wo': _L1_ffn_in['wo'], 'L1_ffn_ln_g': _L1_ffn_in['ln_g'], 'L1_ffn_ln_b': _L1_ffn_in['ln_b'], 'L1_ffn_w1': _L1_ffn_in['w1'], 'L1_ffn_b1': _L1_ffn_in['b1'], 'L1_ffn_w2': _L1_ffn_in['w2'], 'L1_ffn_b2': _L1_ffn_in['b2']}
    _x0 = _d['L0_attn_x']
    _d['L0_attn_x'] = jax.random.normal(jax.random.fold_in(jax.random.key(seed), 1), (2, 2048, 128), dtype=_x0.dtype)
    del _x0
    return _d

def reference(L0_attn_x, L0_attn_W_qkv, L0_attn_b_qkv, L0_ffn_router_w, L0_ffn_w_fc, L0_ffn_w_proj, L0_ffn_shared_fc, L0_ffn_shared_proj, L1_attn_W_q, L1_attn_b_q, L1_attn_W_k, L1_attn_b_k, L1_attn_W_v, L1_attn_b_v, L1_attn_W_a, L1_attn_b_a, L1_ffn_wqkv, L1_ffn_q_scale, L1_ffn_k_scale, L1_ffn_wo, L1_ffn_ln_g, L1_ffn_ln_b, L1_ffn_w1, L1_ffn_b1, L1_ffn_w2, L1_ffn_b2):

    def _L0_attn_ref(x, W_qkv, b_qkv):
        import jax, jax.numpy as jnp
        import numpy as np
        ALPHA = 0.99
        EMBED_DIM = 128
        SEQ_LEN = 256
        BATCH = 4
        bs, sl, d = x.shape
        qkv = x @ W_qkv.T + b_qkv
        q, k, v = jnp.split(qkv, 3, axis=-1)
        idx = jnp.arange(sl)
        diff = (idx[:, None] - idx[None, :]).astype(jnp.float32)
        M = jnp.where(idx[:, None] >= idx[None, :], ALPHA ** diff, 0.0)
        dim_sqrt = jnp.float32(np.sqrt(d))
        scores = jnp.einsum('bqd,bkd->bqk', q, k) / dim_sqrt * M
        out = scores @ v
        return out

    def _L0_ffn_ref(x, router_w, w_fc, w_proj, shared_fc, shared_proj):
        import jax, jax.numpy as jnp
        import numpy as np
        TOP_K = 2

        def _mlp(x, w_fc, w_proj):
            return jnp.square(jax.nn.relu(x @ w_fc.T)) @ w_proj.T
        B, S, D = x.shape
        E = router_w.shape[0]
        T = B * S
        flat = x.reshape(T, D)
        logits = flat @ router_w.T
        probs = jax.nn.softmax(logits.astype(jnp.float32), axis=-1)
        topk_p, topk_i = jax.lax.top_k(probs, TOP_K)
        topk_w = (topk_p / jnp.maximum(topk_p.sum(-1, keepdims=True), 1e-09)).astype(flat.dtype)
        combine = jnp.zeros((T, E), dtype=flat.dtype)
        combine = combine.at[jnp.arange(T)[:, None], topk_i].add(topk_w)
        out = jnp.zeros_like(flat)
        for e in range(E):
            out = out + _mlp(flat, w_fc[e], w_proj[e]) * combine[:, e:e + 1]
        out = out + _mlp(flat, shared_fc, shared_proj)
        return out.reshape(B, S, D)

    def _L1_attn_ref(x_seq, W_q, b_q, W_k, b_k, W_v, b_v, W_a, b_a):
        import jax, jax.numpy as jnp
        import numpy as np
        B, T, D = (4, 512, 128)
        EPS = 1e-06
        q = jax.nn.relu(x_seq @ W_q.T + b_q)
        k = jax.nn.relu(x_seq @ W_k.T + b_k)
        v = x_seq @ W_v.T + b_v
        A = jax.nn.sigmoid(x_seq @ W_a.T + b_a)
        log_g = jax.lax.cumsum(jnp.log(A + 1e-06), axis=1, reverse=True)
        wk = k * jnp.exp(log_g)
        scores = jnp.einsum('btd,bsd->bts', q, wk)
        Tn = x_seq.shape[1]
        mask = jnp.tril(jnp.ones((Tn, Tn), bool))
        scores = jnp.where(mask, scores, 0.0)
        num = jnp.einsum('bts,bsd->btd', scores, v)
        denom = scores.sum(-1, keepdims=True) + EPS
        return num / denom

    def _L1_ffn_ref(x, wqkv, q_scale, k_scale, wo, ln_g, ln_b, w1, b1, w2, b2):
        import jax, jax.numpy as jnp
        import numpy as np
        DIM = 128
        DEPTH = 2
        HEADS = 8
        DIM_HEAD = 64
        WINDOW = 64
        INNER = HEADS * DIM_HEAD
        HID = int(DIM * 4 * 2 / 3)
        B, N = (2, 1024)
        QK_SCALE = 8.0

        def shift_token(t):
            t1, t2 = jnp.split(t, 2, axis=-1)
            t2 = jnp.pad(t2, ((0, 0), (1, 0), (0, 0)))[:, :-1]
            return jnp.concatenate([t1, t2], axis=-1)

        def l2norm(t):
            return t / jnp.clip(jnp.linalg.norm(t, axis=-1, keepdims=True), 1e-12)

        def rotate_half(x):
            x1, x2 = jnp.split(x, 2, axis=-1)
            return jnp.concatenate([-x2, x1], axis=-1)

        def rotary_xpos(q, k):
            n = q.shape[-2]
            half_idx = jnp.arange(0, DIM_HEAD, 2, dtype=jnp.float32)
            inv_freq = 1.0 / 10000.0 ** (half_idx / DIM_HEAD)
            t = jnp.arange(n, dtype=jnp.float32)
            freqs = t[:, None] * inv_freq[None, :]
            freqs = jnp.concatenate([freqs, freqs], axis=-1)
            base = (half_idx + 0.4 * DIM_HEAD) / (1.4 * DIM_HEAD)
            power = (t - n // 2) / float(WINDOW // 2)
            scale = base[None, :] ** power[:, None]
            scale = jnp.concatenate([scale, scale], axis=-1)
            cos, sin = (jnp.cos(freqs), jnp.sin(freqs))
            q = q * cos * scale + rotate_half(q) * sin * scale
            k = k * cos / scale + rotate_half(k) * sin / scale
            return (q, k)

        def local_attention(q, k, v):
            b, h, n, d = q.shape
            w = n // WINDOW
            bq = q.reshape(b, h, w, WINDOW, d) * QK_SCALE
            bk = k.reshape(b, h, w, WINDOW, d)
            bv = v.reshape(b, h, w, WINDOW, d)

            def look_around(t):
                p = jnp.pad(t, ((0, 0), (0, 0), (1, 0), (0, 0), (0, 0)))
                return jnp.concatenate([p[:, :, :w], p[:, :, 1:]], axis=3)
            bk, bv = (look_around(bk), look_around(bv))
            bt = jnp.arange(n).reshape(w, WINDOW)
            btp = jnp.pad(bt, ((1, 0), (0, 0)), constant_values=-1)
            btk = jnp.concatenate([btp[:w], btp[1:]], axis=1)
            sim = jnp.einsum('bhwid,bhwjd->bhwij', bq, bk)
            i = bt[:, :, None]
            j = btk[:, None, :]
            mask = (i < j) | (i > j + WINDOW) | (j == -1)
            sim = jnp.where(mask, -jnp.finfo(sim.dtype).max, sim)
            attn = jax.nn.softmax(sim, axis=-1)
            out = jnp.einsum('bhwij,bhwjd->bhwid', attn, bv)
            return out.reshape(b, h, n, d)

        def _layer(x, wqkv, qs, ksc, wo, lg, lb, w1, b1, w2, b2):
            b, n, _ = x.shape
            h = shift_token(x)
            qkv = h @ wqkv
            q, k, v = jnp.split(qkv, 3, axis=-1)
            to_heads = lambda t: t.reshape(b, n, HEADS, DIM_HEAD).transpose(0, 2, 1, 3)
            q, k, v = (to_heads(q), to_heads(k), to_heads(v))
            q = l2norm(q) * qs
            k = l2norm(k) * ksc
            q, k = rotary_xpos(q, k)
            o = local_attention(q, k, v)
            o = o.transpose(0, 2, 1, 3).reshape(b, n, INNER)
            x = x + o @ wo
            h = shift_token(x)
            mu = h.mean(-1, keepdims=True)
            var = h.var(-1, keepdims=True)
            h = (h - mu) / jnp.sqrt(var + 1e-05) * lg + lb
            h = h @ w1 + b1
            a, g = jnp.split(h, 2, axis=-1)
            h = a * jax.nn.gelu(g, approximate=False)
            x = x + h @ w2 + b2
            return x
        for l in range(DEPTH):
            x = _layer(x, wqkv[l], q_scale[l], k_scale[l], wo[l], ln_g[l], ln_b[l], w1[l], b1[l], w2[l], b2[l])
        return x
    x = L0_attn_x
    x = x + _layernorm(_L0_attn_ref(_layernorm(x, axis=-1), L0_attn_W_qkv, L0_attn_b_qkv), axis=-1)
    x = x + _layernorm(_L0_ffn_ref(_layernorm(x, axis=-1), L0_ffn_router_w, L0_ffn_w_fc, L0_ffn_w_proj, L0_ffn_shared_fc, L0_ffn_shared_proj), axis=-1)
    x = x + _layernorm(_L1_attn_ref(_layernorm(x, axis=-1), L1_attn_W_q, L1_attn_b_q, L1_attn_W_k, L1_attn_b_k, L1_attn_W_v, L1_attn_b_v, L1_attn_W_a, L1_attn_b_a), axis=-1)
    x = x + _layernorm(_L1_ffn_ref(_layernorm(x, axis=-1), L1_ffn_wqkv, L1_ffn_q_scale, L1_ffn_k_scale, L1_ffn_wo, L1_ffn_ln_g, L1_ffn_ln_b, L1_ffn_w1, L1_ffn_b1, L1_ffn_w2, L1_ffn_b2), axis=-1)
    return x

_drawn_inputs = setup_inputs


def setup_inputs(seed=0):
    import zlib

    import numpy as np

    out = dict(_drawn_inputs(seed))
    spreads = {'L1_ffn_q_scale': (1.0, 0.6),
     'L1_ffn_k_scale': (1.0, 0.6),
     'L1_ffn_ln_g': (1.0, 0.6),
     'L1_ffn_ln_b': (0.0, 0.8),
     'L1_ffn_b1': (0.0, 0.8),
     'L1_ffn_b2': (0.0, 0.8)}
    factors = {'L1_attn_W_q': 6.787,
     'L1_attn_b_q': 179.892,
     'L1_attn_W_k': 4.305,
     'L1_attn_b_k': 64.0,
     'L1_attn_b_v': 5.725,
     'L1_attn_W_a': 8.0,
     'L1_attn_b_a': 24.754,
     'L1_ffn_wqkv': 3.671,
     'L1_ffn_wo': 3.713,
     'L1_ffn_w1': 8.0,
     'L1_ffn_w2': 8.0}
    for name, (base, spread) in spreads.items():
        noise = np.random.default_rng([zlib.crc32(name.encode()), seed]).standard_normal(out[name].shape)
        drawn = base * np.exp(spread * noise) if base else spread * noise
        out[name] = jnp.asarray(drawn.astype(out[name].dtype))
    for name, factor in factors.items():
        out[name] = (out[name] * factor).astype(out[name].dtype)
    return out
```

```python
from contextlib import ExitStack

import numpy as np
import concourse.bass as bass
from concourse import mybir

ALU = mybir.AluOpType
ACT = mybir.ActivationFunctionType
F32 = mybir.dt.float32
BF16 = mybir.dt.bfloat16
AX = mybir.AxisListType.X

P = 128
B, N = 2, 2048
G = 512
NIT = N // G
NC = G // P
E, FF = 8, 512
NF = FF // P
NE = E + 1
H, DH, W = 8, 64, 64
INNER = H * DH
NM = INNER // P
DEPTH = 2
HID = 341
HC = [P, P, HID - 2 * P]
ALPHA = 0.99
NEG = -1.0e30
LN_EXP = "natural_log_exp_and_others"
STAGES = 4


def constants():
    i = np.arange(P)
    c = {}
    c["ident"] = np.eye(P, dtype=np.float32)
    c["mean_w"] = np.full((P, P), 1.0 / P, np.float32)
    d = i[None, :] - i[:, None]
    c["decay"] = (np.where(d >= 0, ALPHA ** np.maximum(d, 0), 0.0) / np.sqrt(P)).astype(np.float32)
    c["qdecay"] = np.broadcast_to(ALPHA ** (i + 1.0) / np.sqrt(P), (P, P)).astype(np.float32)
    c["kdecay"] = (ALPHA ** (P - 1.0 - i)).astype(np.float32)[:, None]
    c["causal"] = (d >= 0).astype(np.float32)
    c["pair_ones"] = np.kron(np.eye(2), np.ones((DH, DH))).astype(np.float32)
    c["rank"] = np.broadcast_to(E - np.arange(E, dtype=np.float32), (P, NC, E)).copy()
    q = np.arange(W)[:, None]
    k = np.arange(W)[None, :]
    own = np.where(k <= q, 0.0, NEG)
    before = np.where(k >= q, 0.0, NEG)
    rest = np.concatenate([np.concatenate([own, before], 1), np.concatenate([before, own], 1)], 0)
    first = rest.copy()
    first[:W, W:] = NEG
    c["band"] = np.stack([np.tile(first, (1, 4)), np.tile(rest, (1, 4))], 1).astype(np.float32)
    half = np.arange(0, DH, 2, dtype=np.float32)
    inv = (1.0 / np.float32(10000.0) ** (half / np.float32(DH))).astype(np.float32)
    t = np.arange(N, dtype=np.float32)
    fr = (t[:, None] * inv[None, :]).astype(np.float32)
    base = ((half + np.float32(0.4 * DH)) / np.float32(1.4 * DH)).astype(np.float32)
    power = ((t - N // 2) / np.float32(W // 2)).astype(np.float32)
    sc = base.astype(np.float64)[None, :] ** power.astype(np.float64)[:, None]
    cos, sin = np.cos(fr.astype(np.float64)), np.sin(fr.astype(np.float64))

    def lay(m, signed):
        a = np.concatenate([-m if signed else m, m], 1)
        return np.concatenate([a, a], 1).T

    c["rot"] = np.stack([lay(cos * sc, False), lay(sin * sc, True), lay(cos / sc, False), lay(sin / sc, True)], 1).astype(np.float32)
    return c


def sandwich_kernel(nc, a, out):
    with ExitStack() as ctx:
        def sb(name, shape, dt=F32):
            return ctx.enter_context(nc.sbuf_tensor(name, shape, dt))

        def sem(name):
            return ctx.enter_context(nc.semaphore(name))

        def sems(phase, names):
            return {n: [nc.alloc_semaphore(f"{phase}_{n}_{b}") for b in range(B)] for n in names.split()}

        def release(S):
            nc.clear_and_free_semaphores([s for pair in S.values() for s in pair])
            nc.all_engine_barrier()

        bank = [[ctx.enter_context(nc.psum_tensor(f"bank{b}{i}", [P, G], F32)) for i in range(4)] for b in range(B)]

        x = sb("x", [P, B, N])
        ident = sb("ident", [P, P])
        ident_bf = sb("ident_bf", [P, P], BF16)
        mean_w = sb("mean_w", [P, P])
        decay = sb("decay", [P, P])
        qdecay = sb("qdecay", [P, P])
        kdecay = sb("kdecay", [P, 1])
        eps = sb("eps", [P, 1])
        cen = {w: sb(f"{w}_cen", [P, B, G]) for w in ("pre", "post")}
        sq = {w: sb(f"{w}_sq", [P, B, G]) for w in ("pre", "post")}
        xn = {w: sb(f"{w}_xn", [P, B, G]) for w in ("pre", "post")}
        br = sb("br", [P, B, G])
        WL = 2 * 8 * P + 2 * INNER + 2 * HID + 3 * P
        M_STORE = 2 * NE * FF
        M_LAYERS = M_STORE + 18432
        M_END = M_LAYERS + DEPTH * WL
        mem = sb("mem", [P, M_END + NC * G + NIT * G // 2])
        arena = mem[:, 0:M_STORE]
        store = mem[:, M_STORE:M_LAYERS]

        def over_chunks(t):
            return t[:, None, :].to_broadcast([P, NC, t.shape[-1]])

        LN = "in mean cen sq var rstd out"

        def ln_names(pre):
            return " ".join(f"{pre}_{s}" for s in LN.split())

        def ln_pe_mean(pe, S, pre, b, n, src, psum):
            pe.wait_ge(S[f"{pre}_in"][b], n)
            nc.tensor.matmul(psum[:, :], mean_w[:, :], src, start=True, stop=True).then_inc(S[f"{pre}_mean"][b], 1)

        def ln_pe_var(pe, S, pre, b, n, psum, scratch=None):
            pe.wait_ge(S[f"{pre}_sq"][b], n)
            nc.tensor.matmul(psum[:, :], mean_w[:, :], sq[scratch or pre][:, b, :], start=True, stop=True).then_inc(S[f"{pre}_var"][b], 1)

        def ln_dve_center(dve, S, pre, b, n, src, psum, scratch=None):
            dve.wait_ge(S[f"{pre}_mean"][b], n)
            nc.vector.tensor_tensor(cen[scratch or pre][:, b, :], src, psum[:, :], ALU.subtract).then_inc(S[f"{pre}_cen"][b], 1)

        def ln_act_square(act, S, pre, b, n, scratch=None):
            act.wait_ge(S[f"{pre}_cen"][b], n)
            nc.scalar.activation(sq[scratch or pre][:, b, :], cen[scratch or pre][:, b, :], ACT.Square).then_inc(S[f"{pre}_sq"][b], 1)

        def ln_act_rstd(act, S, pre, b, n, psum, scratch=None):
            to = sq[scratch or pre]
            act.wait_ge(S[f"{pre}_var"][b], n)
            nc.scalar.activation(to[:, b, :], psum[:, :], ACT.Ln, bias=eps[:, :]).then_inc(S[f"{pre}_rstd"][b], 1)
            act.wait_ge(S[f"{pre}_rstd"][b], 2 * n - 1)
            nc.scalar.activation(to[:, b, :], to[:, b, :], ACT.Exp, scale=-0.5).then_inc(S[f"{pre}_rstd"][b], 1)

        def ln_dve_scale(dve, S, pre, b, n, dst):
            dve.wait_ge(S[f"{pre}_rstd"][b], 2 * n)
            nc.vector.tensor_tensor(dst, cen[pre][:, b, :], sq[pre][:, b, :], ALU.mult).then_inc(S[f"{pre}_out"][b], 1)

        w_a = store[:, 0:3 * P]
        b_qk = sb("b_qk", [P, 2])
        b_kv = sb("b_kv", [P, 2 * P])
        wfc = arena[:, 0:NE * FF]
        wpj = arena[:, NE * FF:2 * NE * FF].rearrange("p (e f d) -> p e f d", e=NE, f=NF)
        router = sb("router", [P, E])
        rank = sb("rank", [P, NC, E])
        s_loaded = sem("s_loaded")
        s_x = sem("s_x")
        s_moe = sem("s_moe")
        s_set = sem("s_set")
        s_layers = sem("s_layers")
        s_band = sem("s_band")
        wl = mem[:, M_LAYERS:M_END].rearrange("p (l w) -> p l w", l=DEPTH)
        vec = sb("vec", [P, DEPTH, 13])
        pair_ones = sb("pair_ones", [P, P])
        eps6 = sb("eps6", [P, 1])
        ten_ln2 = sb("ten_ln2", [P, 1])
        zero = sb("zero", [P, 1])
        causal = sb("causal", [P, P])
        w_g = sb("w_g", [P, 4 * P])
        b_g = sb("b_g", [P, 3])
        nb_gate = sb("nb_gate", [P, 1])
        b_v = sb("b_v", [P, P])
        loads0 = [(ident, "ident"), (mean_w, "mean_w"), (decay, "decay"), (qdecay, "qdecay"), (kdecay, "kdecay"), (causal, "causal"),
                  (w_g, "w_gT"), (b_g, "b_gT")]

        with nc.Block() as block:
            @block.sync
            def _(sp):
                for b in range(B):
                    sp.dma_start(x[:, b, :], a["xT"][:, b * N:(b + 1) * N]).then_inc(s_x, 16)
                for t, name in loads0:
                    sp.dma_start(t[:, :], a[name]).then_inc(s_loaded, 16)
                sp.dma_start(w_a, a["wqkvT"]).then_inc(s_loaded, 16)
                sp.dma_start(b_qk[:, :], a["b_qkT"]).then_inc(s_loaded, 16)
                sp.dma_start(b_kv[:, :], a["b_kv"].to_broadcast([P, 2 * P])).then_inc(s_loaded, 16)
                sp.dma_start(router[:, :], a["routerT"]).then_inc(s_loaded, 16)
                sp.dma_start(rank[:, :, :], a["rank"]).then_inc(s_loaded, 16)
                sp.dma_start(b_v[:, :], a["b_v"].to_broadcast([P, P])).then_inc(s_loaded, 16)
                sp.wait_ge(s_loaded, 16 * (len(loads0) + 6))
                sp.wait_ge(s_x, 32)
                sp.dma_start(wfc, a["wfcT"]).then_inc(s_moe, 16)
                sp.dma_start(wpj, a["wpjT"]).then_inc(s_moe, 16)
                for l in range(DEPTH):
                    sp.dma_start(wl[:, l, :], a["wl"][l]).then_inc(s_layers, 16)
                sp.dma_start(vec[:, :, :], a["vec"]).then_inc(s_layers, 16)
                sp.dma_start(pair_ones[:, :], a["pair_ones"]).then_inc(s_layers, 16)

            @block.vector
            def _(dve):
                nc.vector.memset(eps[:, :], 1e-5).then_inc(s_set, 1)
                nc.vector.memset(eps6[:, :], 1e-6).then_inc(s_set, 1)
                nc.vector.memset(zero[:, :], 0.0).then_inc(s_set, 1)
                nc.vector.memset(ten_ln2[:, :], float(10 * np.log(2.0))).then_inc(s_set, 1)
                dve.wait_ge(s_loaded, 16 * (len(loads0) + 6))
                nc.vector.tensor_copy(ident_bf[:, :], ident[:, :]).then_inc(s_set, 1)
                nc.vector.tensor_scalar(nb_gate[:, :], b_g[:, 2:3], -1.0, None, ALU.mult).then_inc(s_set, 1)

        S = sems("lin", ln_names("pre") + " qk kv qkT qg kvb kw scores dstate probs state o " + ln_names("post") + " done")
        qT = store[:, 1024:1024 + B * G].rearrange("p (b g) -> p b g", b=B)
        kT = store[:, 2048:2048 + B * G].rearrange("p (b g) -> p b g", b=B)
        qg = store[:, 3072:3072 + B * G].rearrange("p (b g) -> p b g", b=B)
        kv = store[:, 4096:4096 + B * 2 * G].rearrange("p (b c w) -> p b c w", b=B, c=NC)
        kw = store[:, 6144:6144 + B * G].rearrange("p (b c w) -> p b c w", b=B, c=NC)
        pr = store[:, 7168:7168 + B * G].rearrange("p (b c w) -> p b c w", b=B, c=NC)
        st = store[:, 8192:8192 + B * 5 * P].rearrange("p (b c w) -> p b c w", b=B, c=NC + 1)

        def tok(it):
            return bass.ds(it * G, G)

        if STAGES >= 1:
            with nc.Block() as block:
                @block.tensor
                def _(pe):
                    with pe.Fori(0, NIT) as it:
                        n = it + 1
                        for b in range(B):
                            ln_pe_mean(pe, S, "pre", b, n, x[:, b, tok(it)], bank[b][0])
                        for b in range(B):
                            ln_pe_var(pe, S, "pre", b, n, bank[b][1])
                        for b in range(B):
                            pe.wait_ge(S["pre_out"][b], n)
                            nc.tensor.matmul(bank[b][2][:, :], w_a[:, 0:P], xn["pre"][:, b, :], start=True, stop=True)
                            nc.tensor.matmul(bank[b][3][:, :], w_a[:, P:2 * P], xn["pre"][:, b, :], start=True, stop=True
                                             ).then_inc(S["qk"][b], 1)
                            for c in range(NC):
                                mm = nc.tensor.matmul(bank[b][c // 2][:, (c % 2) * 2 * P:(c % 2 + 1) * 2 * P],
                                                      xn["pre"][:, b, c * P:(c + 1) * P], w_a[:, P:3 * P], start=True, stop=True)
                            mm.then_inc(S["kv"][b], 1)
                        for b in range(B):
                            pe.wait_ge(S["qkT"][b], 2 * n)
                            for c in range(NC):
                                cs = slice(c * P, (c + 1) * P)
                                mm = nc.tensor.matmul(bank[b][2][:, cs], kT[:, b, cs], qT[:, b, cs], start=True, stop=True)
                            mm.then_inc(S["scores"][b], 1)
                            pe.wait_ge(S["kvb"][b], 2 * n)
                            pe.wait_ge(S["kw"][b], n)
                            for c in range(NC):
                                mm = nc.tensor.matmul(bank[b][3][:, c * P:(c + 1) * P], kw[:, b, c, :], kv[:, b, c, P:2 * P],
                                                      start=True, stop=True)
                            mm.then_inc(S["dstate"][b], 1)
                        for b in range(B):
                            pe.wait_ge(S["probs"][b], n)
                            pe.wait_ge(S["qg"][b], n)
                            pe.wait_ge(S["state"][b], 5 * n)
                            for c in range(NC):
                                cs = slice(c * P, (c + 1) * P)
                                nc.tensor.matmul(bank[b][0][:, cs], kv[:, b, c, P:2 * P], pr[:, b, c, :], start=True, stop=False)
                                mm = nc.tensor.matmul(bank[b][0][:, cs], st[:, b, c, :], qg[:, b, cs], start=False, stop=True)
                            mm.then_inc(S["o"][b], 1)
                        for b in range(B):
                            ln_pe_mean(pe, S, "post", b, n, br[:, b, :], bank[b][1])
                        for b in range(B):
                            ln_pe_var(pe, S, "post", b, n, bank[b][2])

                @block.vector
                def _(dve):
                    for b in range(B):
                        nc.vector.memset(st[:, b, NC, :], 0.0).then_inc(S["done"][b], 1)
                        dve.wait_ge(S["done"][b], 1)
                    with dve.Fori(0, NIT) as it:
                        n = it + 1
                        for b in range(B):
                            ln_dve_center(dve, S, "pre", b, n, x[:, b, tok(it)], bank[b][0])
                        for b in range(B):
                            ln_dve_scale(dve, S, "pre", b, n, xn["pre"][:, b, :])
                        for b in range(B):
                            dve.wait_ge(S["kv"][b], n)
                            for j in range(2):
                                nc.vector.tensor_tensor(kv[:, b, 2 * j:2 * j + 2, :],
                                                        bank[b][j][:, :].rearrange("p (c w) -> p c w", c=2),
                                                        b_kv[:, None, :].to_broadcast([P, 2, 2 * P]), ALU.add
                                                        ).then_inc(S["kvb"][b], 1)
                        for b in range(B):
                            dve.wait_ge(S["scores"][b], n)
                            nc.vector.tensor_tensor(pr[:, b, :, :], bank[b][2][:, :].rearrange("p (c w) -> p c w", c=NC),
                                                    over_chunks(decay), ALU.mult).then_inc(S["probs"][b], 1)
                            dve.wait_ge(S["dstate"][b], n)
                            nc.vector.tensor_copy(st[:, b, 0, :], st[:, b, NC, :]).then_inc(S["state"][b], 1)
                            for c in range(NC):
                                dve.wait_ge(S["state"][b], it * 5 + 1 + c)
                                nc.vector.scalar_tensor_tensor(st[:, b, c + 1, :], st[:, b, c, :], float(ALPHA ** P),
                                                               bank[b][3][:, c * P:(c + 1) * P], ALU.mult, ALU.add
                                                               ).then_inc(S["state"][b], 1)
                        for b in range(B):
                            ln_dve_center(dve, S, "post", b, n, br[:, b, :], bank[b][1])
                        for b in range(B):
                            dve.wait_ge(S["done"][b], n)
                            ln_dve_scale(dve, S, "post", b, n, xn["post"][:, b, :])

                @block.scalar
                def _(act):
                    nc.scalar.preload_act_table_set(LN_EXP)
                    with act.Fori(0, NIT) as it:
                        n = it + 1
                        for b in range(B):
                            ln_act_square(act, S, "pre", b, n)
                        for b in range(B):
                            ln_act_rstd(act, S, "pre", b, n, bank[b][1])
                        for b in range(B):
                            act.wait_ge(S["qk"][b], n)
                            nc.scalar.activation(qT[:, b, :], bank[b][2][:, :], ACT.Identity, bias=b_qk[:, 0:1]).then_inc(S["qkT"][b], 1)
                            nc.scalar.activation(kT[:, b, :], bank[b][3][:, :], ACT.Identity, bias=b_qk[:, 1:2]).then_inc(S["qkT"][b], 1)
                        for b in range(B):
                            act.wait_ge(S["kvb"][b], 2 * n)
                            nc.scalar.activation(kw[:, b, :, :], kv[:, b, :, 0:P], ACT.Copy, scale=kdecay[:, 0:1]).then_inc(S["kw"][b], 1)
                        for b in range(B):
                            act.wait_ge(S["o"][b], n)
                            nc.scalar.activation(br[:, b, :], bank[b][0][:, :], ACT.Copy).then_inc(S["post_in"][b], 1)
                        for b in range(B):
                            ln_act_square(act, S, "post", b, n)
                        for b in range(B):
                            ln_act_rstd(act, S, "post", b, n, bank[b][2])

                @block.gpsimd
                def _(pool):
                    for b in range(B):
                        nc.gpsimd.sem_inc(S["pre_in"][b], NIT)
                    with pool.Fori(0, NIT) as it:
                        n = it + 1
                        for b in range(B):
                            pool.wait_ge(S["qkT"][b], 2 * n)
                            nc.gpsimd.tensor_tensor(qg[:, b, :].rearrange("p (c w) -> p c w", c=NC),
                                                    qT[:, b, :].rearrange("p (c w) -> p c w", c=NC), over_chunks(qdecay),
                                                    ALU.mult).then_inc(S["qg"][b], 1)
                        for b in range(B):
                            pool.wait_ge(S["post_out"][b], n)
                            nc.gpsimd.tensor_tensor(x[:, b, tok(it)], x[:, b, tok(it)], xn["post"][:, b, :], ALU.add).then_inc(S["done"][b], 1)

        release(S)
        S = sems("moe", ln_names("pre") + " logits sub expd comb route fc relu hid proj acc accT " + ln_names("post") + " done")
        ROUTE = 21
        relu = store[:, 0:B * NF * G].rearrange("p (b f g) -> p b f g", b=B, f=NF)
        hid = store[:, 4096:4096 + B * NF * G].rearrange("p (b f g) -> p b f g", b=B, f=NF)
        acc = store[:, 8192:8192 + B * NC * P].rearrange("p (b c d) -> p b c d", b=B, c=NC)
        rt = store[:, 9216:9216 + B * 8 * NC * E].rearrange("p (b k c e) -> p b k c e", b=B, k=8, c=NC)
        rs = store[:, 10240:10240 + B * 8 * NC].rearrange("p (b k c) -> p b k c", b=B, k=8)
        ORDER = [E] + list(range(E))

        if STAGES >= 2:
            with nc.Block() as block:
                @block.tensor
                def _(pe):
                    pe.wait_ge(s_moe, 32)
                    with pe.Fori(0, NIT) as it:
                        n = it + 1
                        for b in range(B):
                            ln_pe_mean(pe, S, "pre", b, n, x[:, b, tok(it)], bank[b][0])
                        for b in range(B):
                            ln_pe_var(pe, S, "pre", b, n, bank[b][1])
                        for b in range(B):
                            pe.wait_ge(S["pre_out"][b], n)
                            for c in range(NC):
                                mm = nc.tensor.matmul(bank[b][3][:, c * E:(c + 1) * E], xn["pre"][:, b, c * P:(c + 1) * P],
                                                      router[:, :], start=True, stop=True)
                            mm.then_inc(S["logits"][b], 1)
                        for k, e in enumerate(ORDER):
                            for b in range(B):
                                for j in range(NF):
                                    if k or j >= 2:
                                        pe.wait_ge(S["relu"][b], it * NE * NF + k * NF + j - 1)
                                    nc.tensor.matmul(bank[b][j % 2][:, :], wfc[:, e * FF + j * P:e * FF + (j + 1) * P],
                                                     xn["pre"][:, b, :], start=True, stop=True).then_inc(S["fc"][b], 1)
                            for b in range(B):
                                if k:
                                    pe.wait_ge(S["acc"][b], it * NE + k)
                                pe.wait_ge(S["hid"][b], it * NE * NF + (k + 1) * NF)
                                for c in range(NC):
                                    for j in range(NF):
                                        mm = nc.tensor.matmul(bank[b][2][:, c * P:(c + 1) * P], hid[:, b, j, c * P:(c + 1) * P],
                                                              wpj[:, e, j, :], start=(j == 0), stop=(j == NF - 1))
                                mm.then_inc(S["proj"][b], 1)
                        for b in range(B):
                            pe.wait_ge(S["acc"][b], it * NE + NE)
                            for c in range(NC):
                                mm = nc.tensor.transpose(bank[b][3][:, c * P:(c + 1) * P], acc[:, b, c, :], ident[:, :])
                            mm.then_inc(S["accT"][b], 1)
                        for b in range(B):
                            ln_pe_mean(pe, S, "post", b, n, br[:, b, :], bank[b][2])
                        for b in range(B):
                            ln_pe_var(pe, S, "post", b, n, bank[b][3])

                @block.vector
                def _(dve):
                    def route(b, it):
                        done = [0]

                        def step(ins):
                            done[0] += 1
                            ins.then_inc(S["route"][b], 1)
                            dve.wait_ge(S["route"][b], it * ROUTE + done[0])

                        def spread(k):
                            return rs[:, b, k, :][:, :, None].to_broadcast([P, NC, E])

                        def pick(prob, m, eq, t, k, hot):
                            step(nc.vector.tensor_reduce(rs[:, b, m, :], rt[:, b, prob], AX, ALU.max))
                            step(nc.vector.tensor_tensor(rt[:, b, eq], rt[:, b, prob], spread(m), ALU.is_equal))
                            step(nc.vector.tensor_tensor(rt[:, b, t], rt[:, b, eq], rank[:, :, :], ALU.mult))
                            step(nc.vector.tensor_reduce(rs[:, b, k, :], rt[:, b, t], AX, ALU.max))
                            step(nc.vector.tensor_tensor(rt[:, b, hot], rt[:, b, t], spread(k), ALU.is_equal))

                        logits = bank[b][3][:, 0:NC * E].rearrange("p (c e) -> p c e", c=NC)
                        dve.wait_ge(S["logits"][b], it + 1)
                        step(nc.vector.tensor_reduce(rs[:, b, 0, :], logits, AX, ALU.max))
                        nc.vector.tensor_tensor(rt[:, b, 0], logits, spread(0), ALU.subtract).then_inc(S["sub"][b], 1)
                        dve.wait_ge(S["expd"][b], it + 1)
                        step(nc.vector.tensor_reduce(rs[:, b, 1, :], rt[:, b, 1], AX, ALU.add))
                        step(nc.vector.reciprocal(rs[:, b, 2, :], rs[:, b, 1, :]))
                        step(nc.vector.tensor_tensor(rt[:, b, 2], rt[:, b, 1], spread(2), ALU.mult))
                        pick(2, 3, 3, 3, 4, 4)
                        step(nc.vector.scalar_tensor_tensor(rt[:, b, 5], rt[:, b, 4], -2.0, rt[:, b, 2], ALU.mult, ALU.add))
                        pick(5, 5, 6, 6, 6, 7)
                        step(nc.vector.tensor_tensor(rs[:, b, 7, :], rs[:, b, 3, :], rs[:, b, 5, :], ALU.add))
                        step(nc.vector.tensor_scalar(rs[:, b, 6, :], rs[:, b, 7, :], 1e-9, None, ALU.max))
                        step(nc.vector.reciprocal(rs[:, b, 7, :], rs[:, b, 6, :]))
                        step(nc.vector.tensor_tensor(rt[:, b, 3], rt[:, b, 4], rt[:, b, 7], ALU.add))
                        step(nc.vector.tensor_tensor(rt[:, b, 5], rt[:, b, 3], rt[:, b, 2], ALU.mult))
                        step(nc.vector.tensor_tensor(rt[:, b, 6], rt[:, b, 5], spread(7), ALU.mult))
                        assert done[0] == ROUTE, done[0]

                    with dve.Fori(0, NIT) as it:
                        n = it + 1
                        for b in range(B):
                            ln_dve_center(dve, S, "pre", b, n, x[:, b, tok(it)], bank[b][0])
                        for b in range(B):
                            ln_dve_scale(dve, S, "pre", b, n, xn["pre"][:, b, :])
                        for k, e in enumerate(ORDER):
                            for b in range(B):
                                for j in range(NF):
                                    dve.wait_ge(S["relu"][b], it * NE * NF + k * NF + j + 1)
                                    if k and j == 0:
                                        dve.wait_ge(S["proj"][b], it * NE + k)
                                    nc.vector.tensor_tensor(hid[:, b, j, :], relu[:, b, j, :], relu[:, b, j, :], ALU.mult
                                                            ).then_inc(S["hid"][b], 1)
                            for b in range(B):
                                if k == 1:
                                    route(b, it)
                                dve.wait_ge(S["proj"][b], it * NE + k + 1)
                                if k:
                                    dve.wait_ge(S["acc"][b], it * NE + k)
                                y = bank[b][2]
                                if e == E:
                                    nc.vector.tensor_copy(acc[:, b, :, :], y[:, :].rearrange("p (c d) -> p c d", c=NC)
                                                          ).then_inc(S["acc"][b], 1)
                                else:
                                    for c in range(NC):
                                        ins = nc.vector.scalar_tensor_tensor(acc[:, b, c, :], y[:, c * P:(c + 1) * P],
                                                                             rt[:, b, 6, c, e:e + 1], acc[:, b, c, :],
                                                                             ALU.mult, ALU.add)
                                    ins.then_inc(S["acc"][b], 1)
                        for b in range(B):
                            ln_dve_center(dve, S, "post", b, n, br[:, b, :], bank[b][2])
                        for b in range(B):
                            dve.wait_ge(S["done"][b], n)
                            ln_dve_scale(dve, S, "post", b, n, xn["post"][:, b, :])

                @block.scalar
                def _(act):
                    nc.scalar.preload_act_table_set(LN_EXP)
                    with act.Fori(0, NIT) as it:
                        n = it + 1
                        for b in range(B):
                            ln_act_square(act, S, "pre", b, n)
                        for b in range(B):
                            ln_act_rstd(act, S, "pre", b, n, bank[b][1])
                        for k, e in enumerate(ORDER):
                            for b in range(B):
                                for j in range(NF):
                                    act.wait_ge(S["fc"][b], it * NE * NF + k * NF + j + 1)
                                    if k:
                                        act.wait_ge(S["hid"][b], it * NE * NF + (k - 1) * NF + j + 1)
                                    nc.scalar.activation(relu[:, b, j, :], bank[b][j % 2][:, :], ACT.Relu).then_inc(S["relu"][b], 1)
                            for b in range(B):
                                if k == 1:
                                    act.wait_ge(S["sub"][b], n)
                                    nc.scalar.activation(rt[:, b, 1], rt[:, b, 0], ACT.Exp).then_inc(S["expd"][b], 1)
                        for b in range(B):
                            act.wait_ge(S["accT"][b], n)
                            nc.scalar.activation(br[:, b, :], bank[b][3][:, :], ACT.Copy).then_inc(S["post_in"][b], 1)
                        for b in range(B):
                            ln_act_square(act, S, "post", b, n)
                        for b in range(B):
                            ln_act_rstd(act, S, "post", b, n, bank[b][3])

                @block.gpsimd
                def _(pool):
                    for b in range(B):
                        nc.gpsimd.sem_inc(S["pre_in"][b], NIT)
                        nc.gpsimd.sem_inc(S["done"][b], 1)
                    with pool.Fori(0, NIT) as it:
                        for b in range(B):
                            pool.wait_ge(S["post_out"][b], it + 1)
                            nc.gpsimd.tensor_tensor(x[:, b, tok(it)], x[:, b, tok(it)], xn["post"][:, b, :], ALU.add).then_inc(S["done"][b], 1)

        release(S)
        S = sems("gate", ln_names("pre") + " proj qk expd plus A la v done")
        qs_ = store[:, 0:B * N].rearrange("p (b n) -> p b n", b=B)
        ks_ = store[:, B * N:2 * B * N].rearrange("p (b n) -> p b n", b=B)
        la = store[:, 2 * B * N:3 * B * N].rearrange("p (b n) -> p b n", b=B)
        vs = store[:, 3 * B * N:4 * B * N].rearrange("p (b n) -> p b n", b=B)

        if STAGES >= 3:
            with nc.Block() as block:
                @block.tensor
                def _(pe):
                    with pe.Fori(0, NIT) as it:
                        n = it + 1
                        for b in range(B):
                            ln_pe_mean(pe, S, "pre", b, n, x[:, b, tok(it)], bank[b][0])
                        for b in range(B):
                            ln_pe_var(pe, S, "pre", b, n, bank[b][1])
                        for b in range(B):
                            pe.wait_ge(S["pre_out"][b], n)
                            for j, to in enumerate((2, 3, 0)):
                                nc.tensor.matmul(bank[b][to][:, :], w_g[:, j * P:(j + 1) * P], xn["pre"][:, b, :],
                                                 start=True, stop=True)
                            for c in range(NC):
                                mm = nc.tensor.matmul(bank[b][1][:, c * P:(c + 1) * P], xn["pre"][:, b, c * P:(c + 1) * P],
                                                      w_g[:, 3 * P:4 * P], start=True, stop=True)
                            mm.then_inc(S["proj"][b], 1)
                        for b in range(B):
                            pe.wait_ge(S["expd"][b], n)

                @block.vector
                def _(dve):
                    with dve.Fori(0, NIT) as it:
                        n = it + 1
                        for b in range(B):
                            ln_dve_center(dve, S, "pre", b, n, x[:, b, tok(it)], bank[b][0])
                        for b in range(B):
                            ln_dve_scale(dve, S, "pre", b, n, xn["pre"][:, b, :])
                        for b in range(B):
                            dve.wait_ge(S["proj"][b], n)
                            nc.vector.tensor_tensor(vs[:, b, tok(it)].rearrange("p (c w) -> p c w", c=NC),
                                                    bank[b][1][:, :].rearrange("p (c w) -> p c w", c=NC),
                                                    over_chunks(b_v), ALU.add).then_inc(S["v"][b], 1)
                        for b in range(B):
                            dve.wait_ge(S["expd"][b], n)
                            nc.vector.tensor_scalar(br[:, b, :], br[:, b, :], 1.0, None, ALU.add).then_inc(S["plus"][b], 1)
                            dve.wait_ge(S["plus"][b], n)
                            nc.vector.reciprocal(xn["post"][:, b, :], br[:, b, :]).then_inc(S["A"][b], 1)

                @block.scalar
                def _(act):
                    nc.scalar.preload_act_table_set(LN_EXP)
                    with act.Fori(0, NIT) as it:
                        n = it + 1
                        for b in range(B):
                            ln_act_square(act, S, "pre", b, n)
                        for b in range(B):
                            ln_act_rstd(act, S, "pre", b, n, bank[b][1])
                        for b in range(B):
                            act.wait_ge(S["proj"][b], n)
                            nc.scalar.activation(br[:, b, :], bank[b][0][:, :], ACT.Exp, bias=nb_gate[:, 0:1], scale=-1.0).then_inc(S["expd"][b], 1)
                            nc.scalar.activation(qs_[:, b, tok(it)], bank[b][2][:, :], ACT.Relu, bias=b_g[:, 0:1]).then_inc(S["qk"][b], 1)
                            nc.scalar.activation(ks_[:, b, tok(it)], bank[b][3][:, :], ACT.Relu, bias=b_g[:, 1:2]).then_inc(S["qk"][b], 1)
                        for b in range(B):
                            act.wait_ge(S["A"][b], n)
                            nc.scalar.activation(la[:, b, tok(it)], xn["post"][:, b, :], ACT.Ln, bias=eps6[:, :]).then_inc(S["la"][b], 1)

                @block.gpsimd
                def _(pool):
                    for b in range(B):
                        nc.gpsimd.sem_inc(S["pre_in"][b], NIT)

        release(S)
        S = sems("gla", "sum eL wk vone wkt wktok scores dstate probs state nd plus rec init " + ln_names("post") + " done")
        wkb = arena[:, 0:B * G].rearrange("p (b g) -> p b g", b=B)
        wkt = arena[:, 1024:1024 + B * G].rearrange("p (b c w) -> p b c w", b=B, c=NC)
        vone = arena[:, 2048:2048 + B * NC * 2 * P].rearrange("p (b c w) -> p b c w", b=B, c=NC)
        pr3 = arena[:, 4096:4096 + B * G].rearrange("p (b c w) -> p b c w", b=B, c=NC)
        st3 = arena[:, 5120:5120 + B * 5 * 2 * P].rearrange("p (b c w) -> p b c w", b=B, c=NC + 1)
        ones = arena[:, 7680:7680 + P]

        if STAGES >= 3:
            with nc.Block() as block:
                @block.tensor
                def _(pe):
                    pe.wait_ge(S["init"][1], 1)
                    with pe.Fori(0, NIT) as it:
                        n = it + 1
                        for b in range(B):
                            pe.wait_ge(S["wk"][b], n)
                            for c in range(NC):
                                mm = nc.tensor.transpose(bank[b][0][:, c * P:(c + 1) * P], wkb[:, b, c * P:(c + 1) * P], ident[:, :])
                            mm.then_inc(S["wkt"][b], 1)
                            for c in range(NC):
                                mm = nc.tensor.matmul(bank[b][1][:, c * P:(c + 1) * P], wkb[:, b, c * P:(c + 1) * P],
                                                      qs_[:, b, bass.ds(it * G + c * P, P)], start=True, stop=True)
                            mm.then_inc(S["scores"][b], 1)
                        for b in range(B):
                            pe.wait_ge(S["wktok"][b], n)
                            pe.wait_ge(S["vone"][b], n)
                            for c in range(NC):
                                mm = nc.tensor.matmul(bank[b][2 + c // 2][:, (c % 2) * 2 * P:(c % 2 + 1) * 2 * P],
                                                      wkt[:, b, c, :], vone[:, b, c, :], start=True, stop=True)
                            mm.then_inc(S["dstate"][b], 1)
                        for b in range(B):
                            pe.wait_ge(S["probs"][b], n)
                            pe.wait_ge(S["state"][b], 5 * n)
                            for half, values in ((0, None), (1, ones)):
                                for c in range(NC):
                                    cs = slice(c * P, (c + 1) * P)
                                    v = vone[:, b, c, 0:P] if values is None else values
                                    nc.tensor.matmul(bank[b][half][:, cs], v, pr3[:, b, c, :], start=True, stop=False)
                                    mm = nc.tensor.matmul(bank[b][half][:, cs], st3[:, b, c, half * P:(half + 1) * P],
                                                          qs_[:, b, bass.ds(it * G + c * P, P)], start=False, stop=True)
                            mm.then_inc(S["nd"][b], 1)
                        for b in range(B):
                            ln_pe_mean(pe, S, "post", b, n, br[:, b, :], bank[b][2])
                        for b in range(B):
                            ln_pe_var(pe, S, "post", b, n, bank[b][3])

                @block.vector
                def _(dve):
                    for b in range(B):
                        back = la[:, b, ::-1]
                        nc.vector.tensor_tensor_scan(back, back, zero[:, 0:1].to_broadcast([P, N]), 0.0, ALU.add, ALU.add
                                                     ).then_inc(S["sum"][b], 1)
                    with dve.Fori(0, NIT) as it:
                        n = it + 1
                        for b in range(B):
                            dve.wait_ge(S["eL"][b], n)
                            nc.vector.tensor_tensor(wkb[:, b, :], ks_[:, b, tok(it)], cen["pre"][:, b, :], ALU.mult).then_inc(S["wk"][b], 1)
                        for b in range(B):
                            dve.wait_ge(S["scores"][b], n)
                            nc.vector.tensor_tensor(pr3[:, b, :, :], bank[b][1][:, :].rearrange("p (c w) -> p c w", c=NC),
                                                    over_chunks(causal), ALU.mult).then_inc(S["probs"][b], 1)
                        for b in range(B):
                            dve.wait_ge(S["dstate"][b], n)
                            nc.vector.tensor_copy(st3[:, b, 0, :], st3[:, b, NC, :]).then_inc(S["state"][b], 1)
                            for c in range(NC):
                                dve.wait_ge(S["state"][b], it * 5 + 1 + c)
                                nc.vector.tensor_tensor(st3[:, b, c + 1, :], st3[:, b, c, :],
                                                        bank[b][2 + c // 2][:, (c % 2) * 2 * P:(c % 2 + 1) * 2 * P], ALU.add
                                                        ).then_inc(S["state"][b], 1)
                        for b in range(B):
                            dve.wait_ge(S["nd"][b], n)
                            nc.vector.tensor_scalar(xn["pre"][:, b, :], bank[b][1][:, :], 1e-6, None, ALU.add).then_inc(S["plus"][b], 1)
                            dve.wait_ge(S["plus"][b], n)
                            nc.vector.reciprocal(sq["pre"][:, b, :], xn["pre"][:, b, :]).then_inc(S["rec"][b], 1)
                            dve.wait_ge(S["rec"][b], n)
                            nc.vector.tensor_tensor(br[:, b, :], sq["pre"][:, b, :], bank[b][0][:, :], ALU.mult).then_inc(S["post_in"][b], 1)
                        for b in range(B):
                            ln_dve_center(dve, S, "post", b, n, br[:, b, :], bank[b][2])
                        for b in range(B):
                            dve.wait_ge(S["done"][b], n)
                            ln_dve_scale(dve, S, "post", b, n, xn["post"][:, b, :])

                @block.scalar
                def _(act):
                    nc.scalar.preload_act_table_set(LN_EXP)
                    for b in range(B):
                        act.wait_ge(S["sum"][b], 1)
                    with act.Fori(0, NIT) as it:
                        n = it + 1
                        for b in range(B):
                            nc.scalar.activation(cen["pre"][:, b, :], la[:, b, tok(it)], ACT.Exp).then_inc(S["eL"][b], 1)
                        for b in range(B):
                            act.wait_ge(S["wkt"][b], n)
                            nc.scalar.activation(wkt[:, b, :, :], bank[b][0][:, :].rearrange("p (c w) -> p c w", c=NC), ACT.Copy
                                                 ).then_inc(S["wktok"][b], 1)
                        for b in range(B):
                            ln_act_square(act, S, "post", b, n)
                        for b in range(B):
                            ln_act_rstd(act, S, "post", b, n, bank[b][3])

                @block.gpsimd
                def _(pool):
                    for b in range(B):
                        nc.gpsimd.memset(st3[:, b, NC, :], 0.0).then_inc(S["init"][0], 1)
                        nc.gpsimd.memset(vone[:, b, :, P:2 * P], 1.0).then_inc(S["init"][0], 1)
                    nc.gpsimd.memset(ones, 1.0).then_inc(S["init"][1], 1)
                    for b in range(B):
                        nc.gpsimd.sem_inc(S["done"][b], 1)
                    with pool.Fori(0, NIT) as it:
                        for b in range(B):
                            nc.gpsimd.tensor_copy(vone[:, b, :, 0:P], vs[:, b, tok(it)].rearrange("p (c w) -> p c w", c=NC)
                                                  ).then_inc(S["vone"][b], 1)
                        for b in range(B):
                            pool.wait_ge(S["post_out"][b], it + 1)
                            nc.gpsimd.tensor_tensor(x[:, b, tok(it)], x[:, b, tok(it)], xn["post"][:, b, :], ALU.add).then_inc(S["done"][b], 1)

        release(S)
        LO, HI = slice(0, DH), slice(DH, P)
        o = [0]

        def carve(width):
            o[0] += width
            return mem[:, o[0] - width:o[0]]

        y = [carve(B * (N + 1)).rearrange("p (b n) -> p b n", b=B) for _ in range(2)]
        qr = carve(B * NM * G).rearrange("p (b m g) -> p b m g", b=B, m=NM)
        kr = carve(B * NM * (W + G)).rearrange("p (b m g) -> p b m g", b=B, m=NM)
        vt = carve(B * NC * INNER).rearrange("p (b c w) -> p b c w", b=B, c=NC)
        vb = carve(B * (NC + 1) * INNER).rearrange("p (b c w) -> p b c w", b=B, c=NC + 1)
        y1 = carve(B * (G + 1)).rearrange("p (b g) -> p b g", b=B)
        assert o[0] <= M_LAYERS, o[0]
        rot = mem[:, M_END:M_END + NC * G].rearrange("p (k g) -> p k g", k=4)
        band = mem[:, M_END + NC * G:M_END + NC * G + NIT * G // 2].bitcast(BF16).rearrange("p (k g) -> p k g", k=NIT)
        prob = [cen["pre"], sq["pre"]]
        probT = [cen["post"], sq["post"]]
        oT = xn["post"]
        hs = xn["post"]
        small = sb("small", [P, B, 4, H])

        NU = 2 * B * NC
        S = sems("start", ln_names("pre"))
        if STAGES >= 4:
            with nc.Block() as block:
                @block.sync
                def _(sp):
                    sp.dma_start(rot[:, 0:2, :].rearrange("p k g -> p (k g)"), a["band"].rearrange("p k g -> p (k g)")).then_inc(s_band, 16)

                @block.tensor
                def _(pe):
                    with pe.Fori(0, NIT) as it:
                        n = it + 1
                        for b in range(B):
                            ln_pe_mean(pe, S, "pre", b, n, x[:, b, tok(it)], bank[b][0])
                        for b in range(B):
                            ln_pe_var(pe, S, "pre", b, n, bank[b][1])

                @block.vector
                def _(dve):
                    dve.wait_ge(s_band, 16)
                    nc.vector.tensor_copy(band[:, 0, :], rot[:, 0, :]).then_inc(s_set, 1)
                    for k in range(1, NIT):
                        nc.vector.tensor_copy(band[:, k, :], rot[:, 1, :]).then_inc(s_set, 1)
                    for b in range(B):
                        for l in range(2):
                            nc.vector.memset(y[l][:, b, 0:1], 0.0).then_inc(s_set, 1)
                        nc.vector.memset(vb[:, b, NC, :], 0.0).then_inc(s_set, 1)
                    dve.wait_ge(s_set, 6 + NIT + 3 * B)
                    with dve.Fori(0, NIT) as it:
                        n = it + 1
                        for b in range(B):
                            ln_dve_center(dve, S, "pre", b, n, x[:, b, tok(it)], bank[b][0])
                        for b in range(B):
                            dve.wait_ge(S["pre_rstd"][b], 2 * n)
                            nc.vector.tensor_tensor(y[0][LO, b, bass.ds(it * G, G)], cen["pre"][LO, b, :], sq["pre"][LO, b, :], ALU.mult
                                                    ).then_inc(S["pre_out"][b], 1)
                            nc.vector.tensor_tensor(y[0][HI, b, bass.ds(it * G + 1, G)], cen["pre"][HI, b, :], sq["pre"][HI, b, :], ALU.mult
                                                    ).then_inc(S["pre_out"][b], 1)
                            dve.wait_ge(S["pre_out"][b], 2 * n)

                @block.scalar
                def _(act):
                    nc.scalar.preload_act_table_set(LN_EXP)
                    with act.Fori(0, NIT) as it:
                        n = it + 1
                        for b in range(B):
                            ln_act_square(act, S, "pre", b, n)
                        for b in range(B):
                            ln_act_rstd(act, S, "pre", b, n, bank[b][1])

                @block.gpsimd
                def _(pool):
                    for b in range(B):
                        nc.gpsimd.sem_inc(S["pre_in"][b], NIT)
        release(S)

        for l in range(DEPTH if STAGES >= 4 else 0):
            yin, yout = y[l % 2], y[(l + 1) % 2]
            at = [0]

            def part(width, l=l, at=at):
                at[0] += width
                return wl[:, l, at[0] - width:at[0]]

            w_x = part(8 * P).rearrange("p (m w) -> p m w", m=8)
            w_y = part(8 * P).rearrange("p (m w) -> p m w", m=8)
            w_v = part(INNER)
            w_o = part(INNER).rearrange("p (m w) -> p m w", m=NM)
            w_1 = part(2 * HID)
            w_2 = part(3 * P).rearrange("p (m w) -> p m w", m=3)
            S = sems(f"layer{l}", "nokeys go hcp xy sqr nrm r rotd t3 qk halo v vcp sc0 sc1 mx0 mx1 ex0 ex1 rec0 rec1 pn0 pn1 pt0 pt1 ptc0 ptc1 pv oc wo y1 ln hn ag gl u w2 y2 "
                     + ln_names("mid"))
            s_rot = nc.alloc_semaphore(f"s_rot{l}")
            s_vb = [nc.alloc_semaphore(f"s_vb{l}{b}") for b in range(B)]

            def unit(t):
                return t // 2 % B, t % 2, t // (2 * B)

            with nc.Block() as block:
                @block.sync
                def _(sp):
                    sp.dma_start(rot[:, :, :], a["rot"][:, :, 0:G]).then_inc(s_rot, 16)
                    with sp.Fori(0, NIT) as it:
                        n = it + 1
                        for b in range(B):
                            sp.wait_ge(S["vcp"][b], NC * it + 1)
                            sp.dma_start(vb[HI, b, 0, :], vb[HI, b, NC, :]).then_inc(s_vb[b], 16)
                            sp.wait_ge(s_vb[b], 48 * it + 16)
                            sp.wait_ge(S["vcp"][b], NC * n)
                            sp.dma_start(vb[LO, b, 0:NC, :], vt[LO, b, :, :]).then_inc(s_vb[b], 16)
                            sp.dma_start(vb[HI, b, 1:NC + 1, :], vt[HI, b, :, :]).then_inc(s_vb[b], 16)
                        for b in range(B):
                            sp.wait_ge(S["rotd"][b], 16 * n)
                        sp.dma_start(rot[:, :, :], a["rot"][:, :, bass.ds((n % NIT) * G, G)]).then_inc(s_rot, 16)
                    sp.wait_ge(s_rot, 16 * (NIT + 1))

                @block.tensor
                def _(pe):
                    def scores(b, p, c, band_of_chunk):
                        to = bank[b][p]
                        rows = slice(p * DH, (p + 1) * DH)
                        nc.tensor.matmul(to[:, :], ident_bf[:, :], band_of_chunk, start=True, stop=False, skip_group_check=True)
                        for m in range(NM):
                            q0, k0 = c * P, m * P
                            nc.tensor.matmul(to[LO, k0:k0 + W], qr[rows, b, m, q0:q0 + W], kr[rows, b, m, W + q0:2 * W + q0],
                                             start=False, stop=False, skip_group_check=True)
                            nc.tensor.matmul(to[LO, k0 + W:k0 + P], qr[rows, b, m, q0:q0 + W], kr[rows, b, m, q0:W + q0],
                                             start=False, stop=False, skip_group_check=True)
                            mm = nc.tensor.matmul(to[HI, k0:k0 + P], qr[rows, b, m, q0 + W:q0 + P],
                                                  kr[rows, b, m, W + q0:3 * W + q0], start=False, stop=(m == NM - 1),
                                                  skip_group_check=True)
                        mm.then_inc(S[f"sc{p}"][b], 1)

                    def turn(it, b, p, c):
                        pe.wait_ge(S[f"pn{p}"][b], it * NC + c + 1)
                        for m in range(NM):
                            mm = nc.tensor.transpose(bank[b][p][:, m * P:(m + 1) * P], prob[p][:, b, m * P:(m + 1) * P], ident[:, :])
                        mm.then_inc(S[f"pt{p}"][b], 1)

                    def values(it, b, p, c):
                        pe.wait_ge(S[f"ptc{p}"][b], it * NC + c + 1)
                        rows = slice(p * DH, (p + 1) * DH)
                        for m in range(NM):
                            h0 = (2 * m + p) * DH
                            nc.tensor.matmul(bank[b][2][rows, m * P:m * P + W], vb[:, b, c, h0:h0 + DH],
                                             probT[p][:, b, m * P:m * P + W], start=True, stop=True)
                            mm = nc.tensor.matmul(bank[b][2][rows, m * P + W:(m + 1) * P], vt[:, b, c, h0:h0 + DH],
                                                  probT[p][:, b, m * P + W:(m + 1) * P], start=True, stop=True)
                        if p == 1:
                            mm.then_inc(S["pv"][b], 1)

                    def project(it, b, c):
                        pe.wait_ge(S["oc"][b], it * NC + c + 1)
                        for m in range(NM):
                            mm = nc.tensor.matmul(bank[b][3][:, c * P:(c + 1) * P], w_o[:, m, :], oT[:, b, m * P:(m + 1) * P],
                                                  start=(m == 0), stop=(m == NM - 1))
                        mm.then_inc(S["wo"][b], 1)

                    pe.wait_ge(s_layers, 16 * (DEPTH + 2))
                    with pe.Fori(0, NIT) as it:
                        n = it + 1
                        for m in range(8):
                            for b in range(B):
                                if m:
                                    pe.wait_ge(S["rotd"][b], it * 16 + 2 * m)
                                h = yin[:, b, bass.ds(it * G, G)]
                                nc.tensor.matmul(bank[b][0][:, :], w_x[:, m, :], h, start=True, stop=True)
                                nc.tensor.matmul(bank[b][1][:, :], w_y[:, m, :], h, start=True, stop=True).then_inc(S["xy"][b], 1)
                            for b in range(B):
                                if m == 0:
                                    pe.wait_ge(S["y2"][b], 2 * it + 1)
                                pe.wait_ge(S["sqr"][b], it * 8 + m + 1)
                                nc.tensor.matmul(bank[b][2][:, :], pair_ones[:, :], sq["pre"][:, b, :], start=True, stop=True
                                                 ).then_inc(S["nrm"][b], 1)
                            if m % 2:
                                c = m // 2
                                for b in range(B):
                                    if c == 0:
                                        pe.wait_ge(S["hcp"][b], n)
                                    else:
                                        pe.wait_ge(S["vcp"][b], it * NC + c)
                                    nc.tensor.matmul(bank[b][3][:, :], hs[:, b, c * P:(c + 1) * P], w_v, start=True, stop=True
                                                     ).then_inc(S["v"][b], 1)
                        for b in range(B):
                            pe.wait_ge(S["qk"][b], 8 * n)
                            for p in range(2):
                                scores(b, p, 0, band[:, it, :])
                        for t in range(NU):
                            b, p, c = unit(t)
                            turn(it, b, p, c)
                            if t == 0:
                                for v in range(B):
                                    pe.wait_ge(s_vb[v], 48 * n)
                                    pe.wait_ge(S["vcp"][v], NC * n)
                            else:
                                values(it, *unit(t - 1))
                            if t >= 3 and unit(t - 2)[1] == 1:
                                project(it, unit(t - 2)[0], unit(t - 2)[2])
                            if 1 <= t <= NU - 4:
                                scores(*unit(t + 3), band[:, 1, :])
                        values(it, *unit(NU - 1))
                        project(it, unit(NU - 1)[0], unit(NU - 1)[2])
                        for b in range(B):
                            pe.wait_ge(S["y1"][b], 3 * n)
                            nc.tensor.matmul(bank[b][0][:, :], mean_w[:, :], y1[:, b, 0:G], start=True, stop=True
                                             ).then_inc(S["mid_mean"][b], 1)
                        for b in range(B):
                            ln_pe_var(pe, S, "mid", b, n, bank[b][1], "pre")
                        for j in range(3):
                            for b in range(B):
                                pe.wait_ge(S["hn"][b], n)
                                if j:
                                    pe.wait_ge(S["u"][b], it * 3 + j)
                                nc.tensor.matmul(bank[b][0][0:HC[j], :], w_1[:, j * P:j * P + HC[j]], br[:, b, :], start=True, stop=True)
                                nc.tensor.matmul(bank[b][1][0:HC[j], :], w_1[:, HID + j * P:HID + j * P + HC[j]], br[:, b, :],
                                                 start=True, stop=True).then_inc(S["ag"][b], 1)
                            for b in range(B):
                                pe.wait_ge(S["u"][b], it * 3 + j + 1)
                                mm = nc.tensor.matmul(bank[b][2][:, :], w_2[0:HC[j], j, :], xn["pre"][0:HC[j], b, :],
                                                      start=(j == 0), stop=(j == 2))
                                mm.then_inc(S["w2"][b], 1)

                @block.vector
                def _(dve):
                    for b in range(B):
                        nc.vector.memset(y1[:, b, G:G + 1], 0.0).then_inc(S["y2"][b], 1)
                        dve.wait_ge(S["y2"][b], 1)
                        nc.vector.memset(kr[:, b, :, G:W + G], 0.0).then_inc(S["nokeys"][b], 1)
                    with dve.Fori(0, NIT) as it:
                        n = it + 1
                        dve.wait_ge(s_rot, 16 * n)
                        for m in range(8):
                            s0, t0 = (0, 0) if m < NM else (2, 2)
                            for b in range(B):
                                dve.wait_ge(S["xy"][b], it * 8 + m + 1)
                                if m:
                                    dve.wait_ge(S["qk"][b], it * 8 + m)
                                nc.vector.scalar_tensor_tensor(xn["pre"][:, b, :], bank[b][1][:, :], vec[:, l, s0 + 1:s0 + 2],
                                                               rot[:, t0 + 1, :], ALU.mult, ALU.mult).then_inc(S["rotd"][b], 1)
                                dve.wait_ge(S["sqr"][b], it * 8 + m + 1)
                                nc.vector.scalar_tensor_tensor(cen["pre"][:, b, :], bank[b][0][:, :], vec[:, l, s0:s0 + 1],
                                                               rot[:, t0, :], ALU.mult, ALU.mult).then_inc(S["rotd"][b], 1)
                            for b in range(B):
                                dve.wait_ge(S["t3"][b], it * 8 + m + 1)
                                dve.wait_ge(S["r"][b], (it * 8 + m + 1) * 2)
                                if m == NM:
                                    dve.wait_ge(S["halo"][b], n)
                                to = qr[:, b, m, :] if m < NM else kr[:, b, m - NM, W:W + G]
                                nc.vector.scalar_tensor_tensor(to, cen["post"][:, b, :], 1e12, cen["pre"][:, b, :], ALU.min, ALU.mult
                                                               ).then_inc(S["qk"][b], 1)
                        for t in range(NU + 1):
                            if t:
                                b, p, c = unit(t - 1)
                                hs4 = slice(p * NM, (p + 1) * NM)
                                dve.wait_ge(S[f"ex{p}"][b], it * NC + c + 1)
                                nc.vector.reciprocal(small[:, b, 2, hs4], small[:, b, 1, hs4]).then_inc(S[f"rec{p}"][b], 1)
                                dve.wait_ge(S[f"rec{p}"][b], it * NC + c + 1)
                                v = prob[p][:, b, :].rearrange("p (m k) -> p m k", m=NM)
                                nc.vector.tensor_tensor(v, v, small[:, b, 2, hs4][:, :, None].to_broadcast([P, NM, P]), ALU.mult
                                                        ).then_inc(S[f"pn{p}"][b], 1)
                            if t < NU:
                                b, p, c = unit(t)
                                hs4 = slice(p * NM, (p + 1) * NM)
                                dve.wait_ge(S[f"sc{p}"][b], it * NC + c + 1)
                                nc.vector.tensor_reduce(small[:, b, 3, hs4], bank[b][p][:, :].rearrange("p (m k) -> p m k", m=NM),
                                                        AX, ALU.max).then_inc(S[f"mx{p}"][b], 1)
                                dve.wait_ge(S[f"mx{p}"][b], (it * NC + c) * 2 + 1)
                                nc.vector.tensor_scalar(small[:, b, 0, hs4], small[:, b, 3, hs4], -8.0, None, ALU.mult
                                                        ).then_inc(S[f"mx{p}"][b], 1)
                        for b in range(B):
                            dve.wait_ge(S["wo"][b], NC * n)
                            nc.vector.tensor_copy(y1[HI, b, 0:1], y1[HI, b, G:G + 1]).then_inc(S["y1"][b], 1)
                            dve.wait_ge(S["y1"][b], 3 * it + 1)
                            nc.vector.tensor_tensor(y1[LO, b, 0:G], yin[LO, b, bass.ds(it * G, G)], bank[b][3][LO, :], ALU.add
                                                    ).then_inc(S["y1"][b], 1)
                            nc.vector.tensor_tensor(y1[HI, b, 1:G + 1], yin[HI, b, bass.ds(it * G + 1, G)], bank[b][3][HI, :], ALU.add
                                                    ).then_inc(S["y1"][b], 1)
                            dve.wait_ge(S["y1"][b], 3 * n)
                        for b in range(B):
                            ln_dve_center(dve, S, "mid", b, n, y1[:, b, 0:G], bank[b][0], "pre")
                        for b in range(B):
                            dve.wait_ge(S["mid_rstd"][b], 2 * n)
                            nc.vector.scalar_tensor_tensor(br[:, b, :], cen["pre"][:, b, :], vec[:, l, 4:5], sq["pre"][:, b, :],
                                                           ALU.mult, ALU.mult).then_inc(S["ln"][b], 1)
                            dve.wait_ge(S["ln"][b], n)
                            nc.vector.tensor_scalar(br[:, b, :], br[:, b, :], vec[:, l, 5:6], None, ALU.add).then_inc(S["hn"][b], 1)
                        for j in range(3):
                            for b in range(B):
                                rows = slice(0, HC[j])
                                dve.wait_ge(S["gl"][b], it * 3 + j + 1)
                                if j:
                                    dve.wait_ge(S["w2"][b], it * 3 + j)
                                nc.vector.scalar_tensor_tensor(xn["pre"][rows, b, :], bank[b][0][rows, :], vec[rows, l, 6 + j:7 + j],
                                                               cen["post"][rows, b, :], ALU.add, ALU.mult).then_inc(S["u"][b], 1)
                        for b in range(B):
                            dve.wait_ge(S["w2"][b], 3 * n)
                            nc.vector.scalar_tensor_tensor(yout[LO, b, bass.ds(it * G, G)], bank[b][2][LO, :], vec[LO, l, 12:13],
                                                           y1[LO, b, 0:G], ALU.add, ALU.add).then_inc(S["y2"][b], 1)
                            nc.vector.scalar_tensor_tensor(yout[HI, b, bass.ds(it * G + 1, G)], bank[b][2][HI, :], vec[HI, l, 12:13],
                                                           y1[HI, b, 1:G + 1], ALU.add, ALU.add).then_inc(S["y2"][b], 1)
                            dve.wait_ge(S["y2"][b], 2 * n + 1)

                @block.scalar
                def _(act):
                    nc.scalar.preload_act_table_set(LN_EXP)
                    with act.Fori(0, NIT) as it:
                        n = it + 1
                        for b in range(B):
                            act.wait_ge(S["y2"][b], 2 * it + 1)
                            nc.scalar.activation(hs[:, b, :], yin[:, b, bass.ds(it * G, G)], ACT.Copy).then_inc(S["hcp"][b], 1)
                        for m in range(8):
                            for b in range(B):
                                act.wait_ge(S["xy"][b], it * 8 + m + 1)
                                nc.scalar.activation(sq["pre"][:, b, :], bank[b][0][:, :], ACT.Square).then_inc(S["sqr"][b], 1)
                            for b in range(B):
                                act.wait_ge(S["nrm"][b], it * 8 + m + 1)
                                if m:
                                    act.wait_ge(S["qk"][b], it * 8 + m)
                                nc.scalar.activation(cen["post"][:, b, :], bank[b][2][:, :], ACT.Ln, scale=2.0 ** 20).then_inc(S["r"][b], 1)
                                act.wait_ge(S["r"][b], (it * 8 + m) * 2 + 1)
                                nc.scalar.activation(cen["post"][:, b, :], cen["post"][:, b, :], ACT.Exp, scale=-0.5, bias=ten_ln2[:, :]
                                                     ).then_inc(S["r"][b], 1)
                            if m % 2:
                                c = m // 2
                                for b in range(B):
                                    act.wait_ge(S["v"][b], it * NC + c + 1)
                                    nc.scalar.activation(vt[:, b, c, :], bank[b][3][:, :], ACT.Copy).then_inc(S["vcp"][b], 1)
                        for t in range(NU + 4):
                            if 0 <= t - 3 < NU:
                                b, p, c = unit(t - 3)
                                act.wait_ge(S[f"pt{p}"][b], it * NC + c + 1)
                                nc.scalar.activation(probT[p][:, b, :], bank[b][p][:, :], ACT.Copy).then_inc(S[f"ptc{p}"][b], 1)
                            if t >= 4 and unit(t - 4)[1] == 1:
                                b, p, c = unit(t - 4)
                                act.wait_ge(S["pv"][b], it * NC + c + 1)
                                nc.scalar.activation(oT[:, b, :], bank[b][2][:, :], ACT.Copy).then_inc(S["oc"][b], 1)
                            if t < NU:
                                b, p, c = unit(t)
                                act.wait_ge(S[f"mx{p}"][b], (it * NC + c + 1) * 2)
                                for m in range(NM):
                                    k = p * NM + m
                                    ex = nc.scalar.activation(prob[p][:, b, m * P:(m + 1) * P], bank[b][p][:, m * P:(m + 1) * P],
                                                              ACT.Exp, bias=small[:, b, 0, k:k + 1], scale=8.0,
                                                              accum_out=small[:, b, 1, k:k + 1])
                                ex.then_inc(S[f"ex{p}"][b], 1)
                        for b in range(B):
                            ln_act_square(act, S, "mid", b, n, "pre")
                        for b in range(B):
                            ln_act_rstd(act, S, "mid", b, n, bank[b][1], "pre")
                        nc.scalar.preload_act_table_set("gelu_and_others")
                        for j in range(3):
                            for b in range(B):
                                rows = slice(0, HC[j])
                                act.wait_ge(S["ag"][b], it * 3 + j + 1)
                                if j:
                                    act.wait_ge(S["u"][b], it * 3 + j)
                                nc.scalar.activation(cen["post"][rows, b, :], bank[b][1][rows, :], ACT.Gelu, bias=vec[rows, l, 9 + j:10 + j]
                                                     ).then_inc(S["gl"][b], 1)
                        nc.scalar.preload_act_table_set(LN_EXP)

                @block.gpsimd
                def _(pool):
                    for b in range(B):
                        pool.wait_ge(S["nokeys"][b], 1)
                    with pool.Fori(0, NIT) as it:
                        n = it + 1
                        for b in range(B):
                            pool.wait_ge(S["xy"][b], it * 8 + 1)
                            nc.gpsimd.sem_inc(S["go"][b], 1)
                            nc.gpsimd.tensor_copy(kr[:, b, :, 0:W], kr[:, b, :, G:W + G]).then_inc(S["halo"][b], 1)
                        for m in range(8):
                            for b in range(B):
                                pool.wait_ge(S["rotd"][b], (it * 8 + m + 1) * 2)
                                nc.gpsimd.tensor_tensor(cen["pre"][:, b, :], cen["pre"][:, b, :], xn["pre"][:, b, :], ALU.add
                                                        ).then_inc(S["t3"][b], 1)
            release(S)

        S = sems("end", ln_names("post") + " half done")
        if STAGES >= 4:
            yf = y[DEPTH % 2]
            with nc.Block() as block:
                @block.tensor
                def _(pe):
                    with pe.Fori(0, NIT) as it:
                        n = it + 1
                        for b in range(B):
                            ln_pe_mean(pe, S, "post", b, n, br[:, b, :], bank[b][0])
                        for b in range(B):
                            ln_pe_var(pe, S, "post", b, n, bank[b][1])

                @block.vector
                def _(dve):
                    with dve.Fori(0, NIT) as it:
                        n = it + 1
                        for b in range(B):
                            ln_dve_center(dve, S, "post", b, n, br[:, b, :], bank[b][0])
                        for b in range(B):
                            dve.wait_ge(S["done"][b], n)
                            ln_dve_scale(dve, S, "post", b, n, xn["post"][:, b, :])
                            dve.wait_ge(S["post_out"][b], n)

                @block.scalar
                def _(act):
                    with act.Fori(0, NIT) as it:
                        n = it + 1
                        for b in range(B):
                            act.wait_ge(S["done"][b], n)
                            nc.scalar.activation(br[LO, b, :], yf[LO, b, bass.ds(it * G, G)], ACT.Copy).then_inc(S["half"][b], 1)
                            nc.scalar.activation(br[HI, b, :], yf[HI, b, bass.ds(it * G + 1, G)], ACT.Copy).then_inc(S["post_in"][b], 1)
                        for b in range(B):
                            ln_act_square(act, S, "post", b, n)
                        for b in range(B):
                            ln_act_rstd(act, S, "post", b, n, bank[b][1])

                @block.gpsimd
                def _(pool):
                    for b in range(B):
                        nc.gpsimd.sem_inc(S["done"][b], 1)
                    with pool.Fori(0, NIT) as it:
                        for b in range(B):
                            pool.wait_ge(S["post_out"][b], it + 1)
                            nc.gpsimd.tensor_tensor(x[:, b, tok(it)], x[:, b, tok(it)], xn["post"][:, b, :], ALU.add).then_inc(S["done"][b], 1)

        release(S)
        s_out = sem("s_out")
        with nc.Block() as block:
            @block.sync
            def _(sp):
                sp.wait_ge(s_moe, 32)
                for b in range(B):
                    sp.dma_start(out[:, b * N:(b + 1) * N], x[:, b, :]).then_inc(s_out, 16)
                sp.wait_ge(s_out, 16 * B)


def kernel(**inputs):
    import concourse.bacc as bacc
    from concourse.bass_utils import run_bass_kernel_spmd

    f = {k: np.asarray(v) for k, v in inputs.items()}
    arrays = dict(constants())
    arrays["xT"] = f["L0_attn_x"].reshape(B * N, P).T
    arrays["wqkvT"] = f["L0_attn_W_qkv"].T
    bq = f["L0_attn_b_qkv"]
    arrays["b_qkT"] = bq[:2 * P].reshape(2, P).T
    arrays["b_kv"] = bq[None, P:]
    arrays["w_gT"] = np.concatenate([f[f"L1_attn_W_{n}"].T for n in "qkav"], 1)
    arrays["b_gT"] = np.stack([f[f"L1_attn_b_{n}"] for n in "qka"], 1)
    arrays["b_v"] = f["L1_attn_b_v"][None, :]
    wl = []
    order = np.arange(2 * INNER).reshape(-1, 2, DH // 2)[:, ::-1].reshape(-1)
    for l in range(DEPTH):
        w, wo, w2 = f["L1_ffn_wqkv"][l], f["L1_ffn_wo"][l], f["L1_ffn_w2"][l]
        w2 = np.concatenate([w2, np.zeros((3 * P - HID, P), w2.dtype)], 0)
        wl.append(np.concatenate([w[:, :2 * INNER], w[:, order], w[:, 2 * INNER:],
                                  wo.reshape(NM, P, P).transpose(1, 0, 2).reshape(P, -1), f["L1_ffn_w1"][l],
                                  w2.reshape(3, P, P).transpose(1, 0, 2).reshape(P, -1)], 1))
    arrays["wl"] = np.stack(wl)
    vec = np.zeros((P, DEPTH, 13), np.float32)
    for l in range(DEPTH):
        for i, n in enumerate(("q", "k")):
            s = f[f"L1_ffn_{n}_scale"][l]
            vec[:, l, 2 * i] = np.concatenate([s, s])
            s = np.concatenate([s[DH // 2:], s[:DH // 2]])
            vec[:, l, 2 * i + 1] = np.concatenate([s, s])
        vec[:, l, 4] = f["L1_ffn_ln_g"][l]
        vec[:, l, 5] = f["L1_ffn_ln_b"][l]
        for j in range(3):
            vec[:HC[j], l, 6 + j] = f["L1_ffn_b1"][l, j * P:j * P + HC[j]]
            vec[:HC[j], l, 9 + j] = f["L1_ffn_b1"][l, HID + j * P:HID + j * P + HC[j]]
        vec[:, l, 12] = f["L1_ffn_b2"][l]
    arrays["vec"] = vec
    arrays["routerT"] = f["L0_ffn_router_w"].T
    fc = np.concatenate([f["L0_ffn_w_fc"], f["L0_ffn_shared_fc"][None]], 0)
    pj = np.concatenate([f["L0_ffn_w_proj"], f["L0_ffn_shared_proj"][None]], 0)
    arrays["wfcT"] = fc.reshape(NE * FF, P).T
    arrays["wpjT"] = pj.reshape(NE, P, NF, P).transpose(3, 0, 2, 1)

    nc = bacc.Bacc("TRN2", target_bir_lowering=False, num_devices=1)
    arrays = {k: np.ascontiguousarray(v) for k, v in arrays.items()}
    aps = {k: nc.dram_tensor(f"in_{k}", v.shape, mybir.dt.from_np(v.dtype), kind="ExternalInput").ap() for k, v in arrays.items()}
    out = nc.dram_tensor("out_T", (P, B * N), F32, kind="ExternalOutput").ap()
    sandwich_kernel(nc, aps, out)
    r = run_bass_kernel_spmd(nc, [{f"in_{k}": v for k, v in arrays.items()}], core_ids=[0])
    return np.ascontiguousarray(r.results[0]["out_T"].T).reshape(B, N, P)
```

```python
from contextlib import ExitStack

import numpy as np
import concourse.bass as bass
from concourse import mybir

ALU = mybir.AluOpType
ACT = mybir.ActivationFunctionType
F32 = mybir.dt.float32
BF16 = mybir.dt.bfloat16
F32R = mybir.dt.float32r
AX = mybir.AxisListType.X

P = 128
B, N = 2, 2048
G = 512
NIT = N // G
NC = G // P
E, FF = 8, 512
NF = FF // P
NE = E + 1
H, DH, W = 8, 64, 64
INNER = H * DH
NM = INNER // P
DEPTH = 2
HID = 341
HC = [P, P, HID - 2 * P]
ALPHA = 0.99
NEG = -1.0e30
LN_EXP = "natural_log_exp_and_others"


def constants():
    i = np.arange(P)
    c = {}
    c["ident"] = np.eye(P, dtype=np.float32)
    c["mean_w"] = np.full((P, P), 1.0 / P, np.float32)
    c["center_w"] = (np.eye(P) - 1.0 / P).astype(np.float32)
    d = i[None, :] - i[:, None]
    c["decay"] = (np.where(d >= 0, ALPHA ** np.maximum(d, 0), 0.0) / np.sqrt(P)).astype(np.float32)
    c["qdecay"] = np.broadcast_to(ALPHA ** (i + 1.0) / np.sqrt(P), (P, P)).astype(np.float32)
    c["kdecay"] = (ALPHA ** (P - 1.0 - i)).astype(np.float32)[:, None]
    c["causal"] = (d >= 0).astype(np.float32)
    c["pair_ones"] = np.kron(np.eye(2), np.ones((DH, DH))).astype(np.float32)
    c["rank"] = np.broadcast_to(E - np.arange(E, dtype=np.float32), (P, NC, E)).copy()
    q = np.arange(W)[:, None]
    k = np.arange(W)[None, :]
    own = np.where(k <= q, 0.0, NEG)
    before = np.where(k >= q, 0.0, NEG)
    rest = np.concatenate([np.concatenate([own, before], 1), np.concatenate([before, own], 1)], 0)
    first = rest.copy()
    first[:W, W:] = NEG
    c["band"] = np.stack([np.tile(first, (1, 4)), np.tile(rest, (1, 4))], 1).astype(np.float32)
    half = np.arange(0, DH, 2, dtype=np.float32)
    inv = (1.0 / np.float32(10000.0) ** (half / np.float32(DH))).astype(np.float32)
    t = np.arange(N, dtype=np.float32)
    fr = (t[:, None] * inv[None, :]).astype(np.float32)
    base = ((half + np.float32(0.4 * DH)) / np.float32(1.4 * DH)).astype(np.float32)
    power = ((t - N // 2) / np.float32(W // 2)).astype(np.float32)
    sc = base.astype(np.float64)[None, :] ** power.astype(np.float64)[:, None]
    cos, sin = np.cos(fr.astype(np.float64)), np.sin(fr.astype(np.float64))

    def lay(m, signed):
        a = np.concatenate([-m if signed else m, m], 1)
        return np.concatenate([a, a], 1).T

    c["rot"] = np.stack([lay(cos * sc, False), lay(sin * sc, True), lay(cos / sc, False), lay(sin / sc, True)], 1).astype(np.float32)
    return c


def sandwich_kernel(nc, a, out):
    with ExitStack() as ctx:
        def sb(name, shape, dt=F32):
            return ctx.enter_context(nc.sbuf_tensor(name, shape, dt))

        def sem(name):
            return ctx.enter_context(nc.semaphore(name))

        def sems(phase, names, streams=B):
            return {n: [nc.alloc_semaphore(f"{phase}_{n}_{b}") for b in range(streams)] for n in names.split()}

        def release(S):
            nc.clear_and_free_semaphores([s for pair in S.values() for s in pair])
            nc.all_engine_barrier()

        NS, PASSES = 2 * B, NIT // 2
        bank = [[ctx.enter_context(nc.psum_tensor(f"bank{b}{i}", [P, G], F32)) for i in range(4)] for b in range(B)]

        two = [(bank[t % B][t // B * 2], bank[t % B][t // B * 2 + 1]) for t in range(NS)]

        x = sb("x", [P, B, N])
        ident = sb("ident", [P, P])
        ident_bf = sb("ident_bf", [P, P], BF16)
        mean_w = sb("mean_w", [P, P])
        center_w = sb("center_w", [P, P])
        eps = sb("eps", [P, 1])
        cen = {w: sb(f"{w}_cen", [P, B, G]) for w in ("pre", "post")}
        sq = {w: sb(f"{w}_sq", [P, B, G]) for w in ("pre", "post")}
        xn = {w: sb(f"{w}_xn", [P, B, G]) for w in ("pre", "post")}
        sq4 = [sq[w][:, b, :] for w in sq for b in range(B)]
        cen4 = [cen[w][:, b, :] for w in cen for b in range(B)]
        xn4 = [xn[w][:, b, :] for w in xn for b in range(B)]

        def tok(it):
            return bass.ds(it * G, G)

        def group(it, t):
            return t % B, bass.ds((2 * it + t // B) * G, G)

        KEPT, INPUT = INNER + 2 * HID + 3 * P, 2 * 8 * P + INNER
        wl = sb("wl", [P, DEPTH, KEPT])
        wi_hi, wi_lo = (sb(name, [P, INPUT], F32R) for name in ("wi_hi", "wi_lo"))

        def scope():
            stack = ctx.enter_context(ExitStack())
            return stack, lambda name, shape, dt=F32: stack.enter_context(nc.sbuf_tensor(name, shape, dt))

        def over_chunks(t):
            return t[:, None, :].to_broadcast([P, NC, t.shape[-1]])

        def product(to, w_hi, w_lo, x_hi, x_lo):
            nc.tensor.matmul(to, w_hi, x_hi, start=True, stop=False)
            nc.tensor.matmul(to, w_hi, x_lo, start=False, stop=False)
            return nc.tensor.matmul(to, w_lo, x_hi, start=False, stop=True)

        LN = "in cen sq var rstd out"

        def ln_names(pre):
            return " ".join(f"{pre}_{s}" for s in LN.split())

        def ln_pe_center(pe, S, pre, t, n, src, psum):
            pe.wait_ge(S[f"{pre}_in"][t], n)
            nc.tensor.matmul(psum[:, :], center_w[:, :], src, start=True, stop=True).then_inc(S[f"{pre}_cen"][t], 1)

        def ln_act_square(act, S, pre, t, n, psum, to):
            act.wait_ge(S[f"{pre}_cen"][t], n)
            nc.scalar.activation(to, psum[:, :], ACT.Square).then_inc(S[f"{pre}_sq"][t], 1)

        def ln_pe_var(pe, S, pre, t, n, psum, squares):
            pe.wait_ge(S[f"{pre}_sq"][t], n)
            nc.tensor.matmul(psum[:, :], mean_w[:, :], squares, start=True, stop=True).then_inc(S[f"{pre}_var"][t], 1)

        def ln_act_rstd(act, S, pre, t, n, psum, to):
            act.wait_ge(S[f"{pre}_var"][t], n)
            nc.scalar.activation(to, psum[:, :], ACT.Ln, bias=eps[:, :]).then_inc(S[f"{pre}_rstd"][t], 1)
            act.wait_ge(S[f"{pre}_rstd"][t], 2 * n - 1)
            nc.scalar.activation(to, to, ACT.Exp, scale=-0.5).then_inc(S[f"{pre}_rstd"][t], 1)

        def ln_dve_scale(dve, S, pre, t, n, dst, psum, rstd):
            dve.wait_ge(S[f"{pre}_rstd"][t], 2 * n)
            nc.vector.tensor_tensor(dst, psum[:, :], rstd, ALU.mult).then_inc(S[f"{pre}_out"][t], 1)

        b_qk = sb("b_qk", [P, 2])
        router = sb("router", [P, E])
        rank = sb("rank", [P, NC, E])
        s_loaded = sem("s_loaded")
        s_later = sem("s_later")
        s_x = sem("s_x")
        s_moe = sem("s_moe")
        s_set = sem("s_set")
        s_layers = sem("s_layers")
        s_input = sem("s_input")
        s_rot = sem("s_rot")
        s_band = sem("s_band")
        vec = sb("vec", [P, DEPTH, 13])
        pair_ones = sb("pair_ones", [P, P])
        eps6 = sb("eps6", [P, 1])
        ten_ln2 = sb("ten_ln2", [P, 1])
        zero = sb("zero", [P, 1])
        causal = sb("causal", [P, P])
        w_g = sb("w_g", [P, 4 * P])
        b_g = sb("b_g", [P, 3])
        nb_gate = sb("nb_gate", [P, 1])
        b_v = sb("b_v", [P, P])
        experts_scope, sbe = scope()
        wfc = sbe("wfc", [P, NE * FF])
        wpj = sbe("wpj", [P, NE, NF, P])
        linear_scope, sbl = scope()
        w_a = sbl("w_a", [P, 3 * P])
        b_kv = sbl("b_kv", [P, 2 * P])
        decay = sbl("decay", [P, P])
        qdecay = sbl("qdecay", [P, P])
        kdecay = sbl("kdecay", [P, 1])
        loads0 = [(ident, "ident"), (mean_w, "mean_w"), (center_w, "center_w"), (decay, "decay"), (qdecay, "qdecay"), (kdecay, "kdecay")]
        loads1 = [(causal, "causal"), (w_g, "w_gT"), (b_g, "b_gT"), (router, "routerT")]
        with nc.Block() as block:
            @block.sync
            def _(sp):
                def load_x(half):
                    for b in range(B):
                        cols = slice(half * N // 2, (half + 1) * N // 2)
                        sp.dma_start(x[:, b, cols], a["xT"][:, b * N:(b + 1) * N][:, cols]).then_inc(s_x, 16)

                load_x(0)
                for t, name in loads0:
                    sp.dma_start(t[:, :], a[name]).then_inc(s_loaded, 16)
                sp.dma_start(w_a[:, :], a["wqkvT"]).then_inc(s_loaded, 16)
                sp.dma_start(b_qk[:, :], a["b_qkT"]).then_inc(s_loaded, 16)
                sp.dma_start(b_kv[:, :], a["b_kv"].to_broadcast([P, 2 * P])).then_inc(s_loaded, 16)
                sp.wait_ge(s_loaded, 16 * (len(loads0) + 3))
                sp.wait_ge(s_x, 16 * B)
                load_x(1)
                for t, name in loads1:
                    sp.dma_start(t[:, :], a[name]).then_inc(s_later, 16)
                sp.dma_start(rank[:, :, :], a["rank"]).then_inc(s_later, 16)
                sp.dma_start(b_v[:, :], a["b_v"].to_broadcast([P, P])).then_inc(s_later, 16)
                sp.dma_start(wfc[:, :], a["wfcT"]).then_inc(s_moe, 16)
                sp.dma_start(wpj[:, :, :, :], a["wpjT"]).then_inc(s_moe, 16)
                for l in range(DEPTH):
                    sp.dma_start(wl[:, l, :], a["wl"][l]).then_inc(s_layers, 16)
                sp.dma_start(vec[:, :, :], a["vec"]).then_inc(s_layers, 16)
                sp.dma_start(pair_ones[:, :], a["pair_ones"]).then_inc(s_layers, 16)

            @block.vector
            def _(dve):
                nc.vector.memset(eps[:, :], 1e-5).then_inc(s_set, 1)
                nc.vector.memset(eps6[:, :], 1e-6).then_inc(s_set, 1)
                nc.vector.memset(zero[:, :], 0.0).then_inc(s_set, 1)
                nc.vector.memset(ten_ln2[:, :], float(10 * np.log(2.0))).then_inc(s_set, 1)
                dve.wait_ge(s_loaded, 16 * (len(loads0) + 3))
                nc.vector.tensor_copy(ident_bf[:, :], ident[:, :]).then_inc(s_set, 1)

        S = sems("lin", ln_names("pre") + " qkT qk qg kv kvb kw scores dstate probs o " + ln_names("post") + " done", NS)
        S |= sems("lin", "state")
        lin = sbl("lin", [P, 5, NS, G])
        qT, kT, qg, kw, pr = ([lin[:, i, t, :] for t in range(NS)] for i in range(5))
        kvs = sbl("kvs", [P, NS, NC, 2 * P])
        kv = [kvs[:, t, :, :] for t in range(NS)]
        NSLOT = 2 * NC + 1
        st = sbl("st", [P, B, NSLOT, P])

        def chunks(t):
            return t.rearrange("p (c w) -> p c w", c=NC)

        with nc.Block() as block:
            @block.tensor
            def _(pe):
                with pe.Fori(0, PASSES) as it:
                    n = it + 1
                    for t in range(NS):
                        b, cols = group(it, t)
                        ln_pe_center(pe, S, "pre", t, n, x[:, b, cols], two[t][0])
                    for t in range(NS):
                        ln_pe_var(pe, S, "pre", t, n, two[t][1], sq4[t])
                    for t in range(NS):
                        pe.wait_ge(S["pre_out"][t], n)
                        nc.tensor.matmul(two[t][0][:, :], w_a[:, 0:P], xn4[t], start=True, stop=True)
                        nc.tensor.matmul(two[t][1][:, :], w_a[:, P:2 * P], xn4[t], start=True, stop=True).then_inc(S["qk"][t], 1)
                    for t in range(NS):
                        pe.wait_ge(S["qkT"][t], 2 * n)
                        for c in range(NC):
                            mm = nc.tensor.matmul(two[t][c // 2][:, (c % 2) * 2 * P:(c % 2 + 1) * 2 * P],
                                                  xn4[t][:, c * P:(c + 1) * P], w_a[:, P:3 * P], start=True, stop=True)
                        mm.then_inc(S["kv"][t], 1)
                    for t in range(NS):
                        pe.wait_ge(S["kvb"][t], 2 * n)
                        for c in range(NC):
                            cs = slice(c * P, (c + 1) * P)
                            mm = nc.tensor.matmul(two[t][0][:, cs], kT[t][:, cs], qT[t][:, cs], start=True, stop=True)
                        mm.then_inc(S["scores"][t], 1)
                        pe.wait_ge(S["kw"][t], n)
                        for c in range(NC):
                            mm = nc.tensor.matmul(two[t][1][:, c * P:(c + 1) * P], kw[t][:, c * P:(c + 1) * P], kv[t][:, c, P:2 * P],
                                                  start=True, stop=True)
                        mm.then_inc(S["dstate"][t], 1)
                    for t in range(NS):
                        pe.wait_ge(S["probs"][t], n)
                        pe.wait_ge(S["qg"][t], n)
                        pe.wait_ge(S["state"][t % B], it * NSLOT + 1 + (t // B + 1) * NC)
                        for c in range(NC):
                            cs = slice(c * P, (c + 1) * P)
                            nc.tensor.matmul(two[t][0][:, cs], kv[t][:, c, P:2 * P], pr[t][:, cs], start=True, stop=False)
                            mm = nc.tensor.matmul(two[t][0][:, cs], st[:, t % B, t // B * NC + c, :], qg[t][:, cs], start=False, stop=True)
                        mm.then_inc(S["o"][t], 1)
                    for t in range(NS):
                        ln_pe_center(pe, S, "post", t, n, cen4[t], two[t][0])
                    for t in range(NS):
                        ln_pe_var(pe, S, "post", t, n, two[t][1], sq4[t])
                    for t in range(NS):
                        pe.wait_ge(S["post_out"][t], n)

            @block.vector
            def _(dve):
                for b in range(B):
                    nc.vector.memset(st[:, b, NSLOT - 1, :], 0.0).then_inc(S["done"][b], 1)
                    nc.vector.memset(st[:, b, 0, :], 0.0).then_inc(S["done"][B + b], 1)
                for t in range(NS):
                    dve.wait_ge(S["done"][t], 1)
                with dve.Fori(0, PASSES) as it:
                    n = it + 1
                    for t in range(NS):
                        dve.wait_ge(S["done"][t], n)
                        ln_dve_scale(dve, S, "pre", t, n, xn4[t], two[t][0], sq4[t])
                    for t in range(NS):
                        dve.wait_ge(S["kv"][t], n)
                        for j in range(2):
                            nc.vector.tensor_tensor(kv[t][:, 2 * j:2 * j + 2, :], two[t][j][:, :].rearrange("p (c w) -> p c w", c=2),
                                                    b_kv[:, None, :].to_broadcast([P, 2, 2 * P]), ALU.add).then_inc(S["kvb"][t], 1)
                    for t in range(NS):
                        b, half = t % B, t // B
                        dve.wait_ge(S["scores"][t], n)
                        nc.vector.tensor_tensor(chunks(pr[t]), chunks(two[t][0][:, :]), over_chunks(decay), ALU.mult
                                                ).then_inc(S["probs"][t], 1)
                        dve.wait_ge(S["dstate"][t], n)
                        if half == 0:
                            nc.vector.tensor_copy(st[:, b, 0, :], st[:, b, NSLOT - 1, :]).then_inc(S["state"][b], 1)
                        for c in range(NC):
                            k = half * NC + c
                            dve.wait_ge(S["state"][b], it * NSLOT + 1 + k)
                            nc.vector.scalar_tensor_tensor(st[:, b, k + 1, :], st[:, b, k, :], float(ALPHA ** P),
                                                           two[t][1][:, c * P:(c + 1) * P], ALU.mult, ALU.add
                                                           ).then_inc(S["state"][b], 1)
                    for t in range(NS):
                        ln_dve_scale(dve, S, "post", t, n, xn4[t], two[t][0], sq4[t])

            @block.scalar
            def _(act):
                nc.scalar.preload_act_table_set(LN_EXP)
                with act.Fori(0, PASSES) as it:
                    n = it + 1
                    for t in range(NS):
                        ln_act_square(act, S, "pre", t, n, two[t][0], sq4[t])
                    for t in range(NS):
                        ln_act_rstd(act, S, "pre", t, n, two[t][1], sq4[t])
                    for t in range(NS):
                        act.wait_ge(S["qk"][t], n)
                        nc.scalar.activation(qT[t], two[t][0][:, :], ACT.Identity, bias=b_qk[:, 0:1]).then_inc(S["qkT"][t], 1)
                        nc.scalar.activation(kT[t], two[t][1][:, :], ACT.Identity, bias=b_qk[:, 1:2]).then_inc(S["qkT"][t], 1)
                    for t in range(NS):
                        act.wait_ge(S["kvb"][t], 2 * n)
                        nc.scalar.activation(chunks(kw[t]), kv[t][:, :, 0:P], ACT.Copy, scale=kdecay[:, 0:1]).then_inc(S["kw"][t], 1)
                    for t in range(NS):
                        act.wait_ge(S["o"][t], n)
                        nc.scalar.activation(cen4[t], two[t][0][:, :], ACT.Copy).then_inc(S["post_in"][t], 1)
                    for t in range(NS):
                        ln_act_square(act, S, "post", t, n, two[t][0], sq4[t])
                    for t in range(NS):
                        ln_act_rstd(act, S, "post", t, n, two[t][1], sq4[t])

            @block.gpsimd
            def _(pool):
                for t in range(NS):
                    nc.gpsimd.sem_inc(S["pre_in"][t], 1)
                pool.wait_ge(s_x, 2 * 16 * B)
                for t in range(NS):
                    nc.gpsimd.sem_inc(S["pre_in"][t], PASSES - 1)
                with pool.Fori(0, PASSES) as it:
                    n = it + 1
                    for t in range(NS):
                        pool.wait_ge(S["qkT"][t], 2 * n)
                        nc.gpsimd.tensor_tensor(chunks(qg[t]), chunks(qT[t]), over_chunks(qdecay), ALU.mult).then_inc(S["qg"][t], 1)
                    for t in range(NS):
                        b, cols = group(it, t)
                        pool.wait_ge(S["post_out"][t], n)
                        nc.gpsimd.tensor_tensor(x[:, b, cols], x[:, b, cols], xn4[t], ALU.add).then_inc(S["done"][t], 1)

        release(S)
        linear_scope.close()
        S = sems("moe", "w_hi w_lo in_hi in_lo pre_cen pre_kept pre_sq pre_var pre_rstd pre_out logits sub expd route fc relu hid proj acc accT "
                 "post_in post_cen post_kept post_sq post_var post_rstd post_out done")
        ROUTE = 21
        br = sbe("br", [P, B, G])
        relu = sbe("relu", [P, B, NF, G])
        hid = sbe("hid", [P, B, NF, G])
        acc = sbe("acc", [P, B, NC, P])
        rt = sbe("rt", [P, B, 8, NC, E])
        rs = sbe("rs", [P, B, 8, NC])
        w_hi, w_lo = (sbe(n, [P, NE * FF], F32R) for n in ("w_hi", "w_lo"))
        in_hi, in_lo = (sbe(n, [P, B, G], F32R) for n in ("in_hi", "in_lo"))
        ORDER = [E] + list(range(E))
        HALVES = range(0, NF // 2), range(NF // 2, NF)
        PRE_CENTER, PRE_VAR = 4, 6

        def started(q):
            return not isinstance(q, int) or q > 0

        with nc.Block() as block:
            @block.tensor
            def _(pe):
                def hidden(b, q, k, chunks=range(NF)):
                    e = ORDER[k]
                    for j in chunks:
                        if started(q) or j >= 2:
                            pe.wait_ge(S["relu"][b], q * NF + j - 1)
                        product(bank[b][j % 2][:, :], w_hi[:, e * FF + j * P:e * FF + (j + 1) * P],
                                w_lo[:, e * FF + j * P:e * FF + (j + 1) * P], in_hi[:, b, :], in_lo[:, b, :]
                                ).then_inc(S["fc"][b], 1)

                def project(b, q, k, part=range(NC)):
                    if part[0] == 0:
                        if started(q):
                            pe.wait_ge(S["acc"][b], q)
                        pe.wait_ge(S["hid"][b], q * NF + NF)
                    for c in part:
                        for j in range(NF):
                            mm = nc.tensor.matmul(bank[b][2][:, c * P:(c + 1) * P], hid[:, b, j, c * P:(c + 1) * P],
                                                  wpj[:, ORDER[k], j, :], start=(j == 0), stop=(j == NF - 1))
                    if part[-1] == NC - 1:
                        mm.then_inc(S["proj"][b], 1)

                def pre_center(b, g, first=False):
                    if not first:
                        pe.wait_ge(S["sub"][b], g)
                    nc.tensor.matmul(bank[b][3][:, :], center_w[:, :], x[:, b, tok(g)], start=True, stop=True
                                     ).then_inc(S["pre_cen"][b], 1)

                def var(w, b, n):
                    pe.wait_ge(S[f"{w}_sq"][b], n)
                    pe.wait_ge(S[f"{w}_kept"][b], n)
                    nc.tensor.matmul(bank[b][3][:, :], mean_w[:, :], sq[w][:, b, :], start=True, stop=True
                                     ).then_inc(S[f"{w}_var"][b], 1)

                def logits(b, n):
                    pe.wait_ge(S["done"][b], n)
                    for c in range(NC):
                        mm = nc.tensor.matmul(bank[b][3][:, c * E:(c + 1) * E], xn["pre"][:, b, c * P:(c + 1) * P],
                                              router[:, :], start=True, stop=True)
                    mm.then_inc(S["logits"][b], 1)

                def experts(g, more):
                    for k in range(1, NE):
                        q = g * NE + k
                        for half in HALVES:
                            hidden(0, q, k, half)
                            project(1, q - 1, k - 1, half)
                        if k == 1:
                            for b in range(B):
                                logits(b, g + 1)
                        for half in HALVES:
                            hidden(1, q, k, half)
                            project(0, q, k, half)
                        for b in range(B):
                            if more and k == PRE_CENTER:
                                pre_center(b, g + 1)
                            if more and k == PRE_VAR:
                                var("pre", b, g + 2)
                    project(1, g * NE + NE - 1, NE - 1)

                def turn(b, g, layernorms):
                    pe.wait_ge(S["acc"][b], g * NE + NE)
                    pe.wait_ge(S["pre_rstd"][b], 2 * layernorms)
                    for c in range(NC):
                        mm = nc.tensor.transpose(bank[b][3][:, c * P:(c + 1) * P], acc[:, b, c, :], ident[:, :])
                    mm.then_inc(S["accT"][b], 1)

                def post_center(b, n):
                    pe.wait_ge(S["post_in"][b], n)
                    nc.tensor.matmul(bank[b][3][:, :], center_w[:, :], br[:, b, :], start=True, stop=True
                                     ).then_inc(S["post_cen"][b], 1)

                pe.wait_ge(s_moe, 32)
                pe.wait_ge(s_later, 16 * (len(loads1) + 2))
                for b in range(B):
                    pre_center(b, 0, first=True)
                for b in range(B):
                    var("pre", b, 1)
                for b in range(B):
                    pe.wait_ge(S["in_lo"][b], 1)
                    pe.wait_ge(S["w_lo"][0], 1)
                    hidden(b, 0, 0)
                project(0, 0, 0)
                pe.wait_ge(S["w_lo"][0], NE)
                with pe.Fori(0, NIT - 1) as it:
                    n = it + 1
                    experts(it, True)
                    for b in range(B):
                        turn(b, it, it + 2)
                        if b == 0:
                            pe.wait_ge(S["in_lo"][0], n + 1)
                            hidden(0, n * NE, 0)
                    for b in range(B):
                        post_center(b, n)
                    pe.wait_ge(S["in_lo"][1], n + 1)
                    hidden(1, n * NE, 0)
                    project(0, n * NE, 0)
                    for b in range(B):
                        var("post", b, n)
                experts(NIT - 1, False)
                for b in range(B):
                    turn(b, NIT - 1, NIT)
                for b in range(B):
                    post_center(b, NIT)
                for b in range(B):
                    var("post", b, NIT)

            @block.vector
            def _(dve):
                def route(b, it):
                    done = [0]

                    def step(ins):
                        done[0] += 1
                        ins.then_inc(S["route"][b], 1)
                        dve.wait_ge(S["route"][b], it * ROUTE + done[0])

                    def spread(k):
                        return rs[:, b, k, :][:, :, None].to_broadcast([P, NC, E])

                    def pick(prob, m, eq, t, k, hot):
                        step(nc.vector.tensor_reduce(rs[:, b, m, :], rt[:, b, prob], AX, ALU.max))
                        step(nc.vector.tensor_tensor(rt[:, b, eq], rt[:, b, prob], spread(m), ALU.is_equal))
                        step(nc.vector.tensor_tensor(rt[:, b, t], rt[:, b, eq], rank[:, :, :], ALU.mult))
                        step(nc.vector.tensor_reduce(rs[:, b, k, :], rt[:, b, t], AX, ALU.max))
                        step(nc.vector.tensor_tensor(rt[:, b, hot], rt[:, b, t], spread(k), ALU.is_equal))

                    logits = bank[b][3][:, 0:NC * E].rearrange("p (c e) -> p c e", c=NC)
                    dve.wait_ge(S["logits"][b], it + 1)
                    step(nc.vector.tensor_reduce(rs[:, b, 0, :], logits, AX, ALU.max))
                    nc.vector.tensor_tensor(rt[:, b, 0], logits, spread(0), ALU.subtract).then_inc(S["sub"][b], 1)
                    dve.wait_ge(S["expd"][b], it + 1)
                    step(nc.vector.tensor_reduce(rs[:, b, 1, :], rt[:, b, 1], AX, ALU.add))
                    step(nc.vector.reciprocal(rs[:, b, 2, :], rs[:, b, 1, :]))
                    step(nc.vector.tensor_tensor(rt[:, b, 2], rt[:, b, 1], spread(2), ALU.mult))
                    pick(2, 3, 3, 3, 4, 4)
                    step(nc.vector.scalar_tensor_tensor(rt[:, b, 5], rt[:, b, 4], -2.0, rt[:, b, 2], ALU.mult, ALU.add))
                    pick(5, 5, 6, 6, 6, 7)
                    step(nc.vector.tensor_tensor(rs[:, b, 7, :], rs[:, b, 3, :], rs[:, b, 5, :], ALU.add))
                    step(nc.vector.tensor_scalar(rs[:, b, 6, :], rs[:, b, 7, :], 1e-9, None, ALU.max))
                    step(nc.vector.reciprocal(rs[:, b, 7, :], rs[:, b, 6, :]))
                    step(nc.vector.tensor_tensor(rt[:, b, 3], rt[:, b, 4], rt[:, b, 7], ALU.add))
                    step(nc.vector.tensor_tensor(rt[:, b, 5], rt[:, b, 3], rt[:, b, 2], ALU.mult))
                    step(nc.vector.tensor_tensor(rt[:, b, 6], rt[:, b, 5], spread(7), ALU.mult))
                    assert done[0] == ROUTE, done[0]
                dve.wait_ge(s_later, 16 * (len(loads1) + 2))
                nc.vector.tensor_scalar(nb_gate[:, :], b_g[:, 2:3], -1.0, None, ALU.mult).then_inc(s_set, 1)

                def square(b, q, chunks=range(NF)):
                    for j in chunks:
                        dve.wait_ge(S["relu"][b], q * NF + j + 1)
                        if started(q) and j == 0:
                            dve.wait_ge(S["proj"][b], q)
                        nc.vector.tensor_tensor(hid[:, b, j, :], relu[:, b, j, :], relu[:, b, j, :], ALU.mult
                                                ).then_inc(S["hid"][b], 1)

                def keep(w, b, n):
                    dve.wait_ge(S[f"{w}_sq"][b], n)
                    nc.vector.tensor_copy(cen[w][:, b, :], bank[b][3][:, :]).then_inc(S[f"{w}_kept"][b], 1)

                def scale(w, b, n):
                    dve.wait_ge(S[f"{w}_rstd"][b], 2 * n)
                    nc.vector.tensor_tensor(xn[w][:, b, :], cen[w][:, b, :], sq[w][:, b, :], ALU.mult
                                            ).then_inc(S[f"{w}_out"][b], 1)

                def rest(b, n):
                    dve.wait_ge(S["in_hi"][b], n)
                    nc.vector.tensor_tensor(in_lo[:, b, :], xn["pre"][:, b, :], in_hi[:, b, :].bitcast(F32), ALU.subtract
                                            ).then_inc(S["in_lo"][b], 1)

                def start_sum(b, q, g):
                    dve.wait_ge(S["proj"][b], q + 1)
                    if started(q):
                        dve.wait_ge(S["accT"][b], g)
                        dve.wait_ge(S["acc"][b], q)
                    nc.vector.tensor_copy(acc[:, b, :, :], bank[b][2][:, :].rearrange("p (c d) -> p c d", c=NC)
                                          ).then_inc(S["acc"][b], 1)

                def combine(b, g, k):
                    q = g * NE + k
                    if k == 0:
                        start_sum(b, q, g)
                        return
                    if k == 1:
                        route(b, g)
                    dve.wait_ge(S["proj"][b], q + 1)
                    dve.wait_ge(S["acc"][b], q)
                    for c in range(NC):
                        ins = nc.vector.scalar_tensor_tensor(acc[:, b, c, :], bank[b][2][:, c * P:(c + 1) * P],
                                                             rt[:, b, 6, c, ORDER[k]:ORDER[k] + 1], acc[:, b, c, :],
                                                             ALU.mult, ALU.add)
                    ins.then_inc(S["acc"][b], 1)

                def experts(g, more):
                    for k in range(1, NE):
                        q = g * NE + k
                        square(0, q)
                        combine(1, g, k - 1)
                        square(1, q)
                        for b in range(B):
                            if more and k == PRE_CENTER + 1:
                                keep("pre", b, g + 2)
                            if more and k == NE - 1:
                                dve.wait_ge(S["fc"][b], (g + 1) * NE * NF)
                                scale("pre", b, g + 2)
                        for b in range(B):
                            if more and k == NE - 1:
                                rest(b, g + 2)
                        combine(0, g, k)
                    combine(1, g, NE - 1)

                for b in range(B):
                    keep("pre", b, 1)
                for b in range(B):
                    scale("pre", b, 1)
                for b in range(B):
                    rest(b, 1)
                for b in range(B):
                    square(b, 0)
                combine(0, 0, 0)
                with dve.Fori(0, NIT - 1) as it:
                    n = it + 1
                    experts(it, True)
                    square(0, n * NE)
                    for b in range(B):
                        keep("post", b, n)
                    square(1, n * NE)
                    combine(0, n, 0)
                    for b in range(B):
                        dve.wait_ge(S["done"][b], n)
                        scale("post", b, n)
                experts(NIT - 1, False)
                for b in range(B):
                    keep("post", b, NIT)
                for b in range(B):
                    dve.wait_ge(S["done"][b], NIT)
                    scale("post", b, NIT)

            @block.scalar
            def _(act):
                nc.scalar.preload_act_table_set(LN_EXP)

                def rectify(b, q, chunks=range(NF)):
                    for j in chunks:
                        act.wait_ge(S["fc"][b], q * NF + j + 1)
                        if started(q):
                            act.wait_ge(S["hid"][b], q * NF + j - NF + 1)
                        nc.scalar.activation(relu[:, b, j, :], bank[b][j % 2][:, :], ACT.Relu).then_inc(S["relu"][b], 1)

                def centred_square(w, b, n):
                    act.wait_ge(S[f"{w}_cen"][b], n)
                    if w == "pre" and started(n - 1):
                        act.wait_ge(S["pre_out"][b], n - 1)
                    nc.scalar.activation(sq[w][:, b, :], bank[b][3][:, :], ACT.Square).then_inc(S[f"{w}_sq"][b], 1)

                def experts(g, more):
                    for k in range(1, NE):
                        for b in range(B):
                            rectify(b, g * NE + k)
                            if k == 1 and b == 1:
                                probabilities(0, g)
                            if k == 2 and b == 0:
                                probabilities(1, g)
                        for b in range(B):
                            if more and k == PRE_CENTER + 1:
                                centred_square("pre", b, g + 2)
                            if more and k == PRE_VAR + 1:
                                ln_act_rstd(act, S, "pre", b, g + 2, bank[b][3], sq["pre"][:, b, :])
                            if more and k == NE - 1:
                                high(b, g + 2)

                def high(b, n):
                    act.wait_ge(S["pre_out"][b], n)
                    nc.scalar.activation(in_hi[:, b, :], xn["pre"][:, b, :], ACT.Copy).then_inc(S["in_hi"][b], 1)

                def high_weights(k):
                    e = slice(ORDER[k] * FF, (ORDER[k] + 1) * FF)
                    nc.scalar.activation(w_hi[:, e], wfc[:, e], ACT.Copy).then_inc(S["w_hi"][0], 1)

                def probabilities(b, g):
                    act.wait_ge(S["sub"][b], g + 1)
                    nc.scalar.activation(rt[:, b, 1], rt[:, b, 0], ACT.Exp).then_inc(S["expd"][b], 1)

                def take(b, n):
                    act.wait_ge(S["accT"][b], n)
                    nc.scalar.activation(br[:, b, :], bank[b][3][:, :], ACT.Copy).then_inc(S["post_in"][b], 1)

                act.wait_ge(s_moe, 32)
                high_weights(0)
                for b in range(B):
                    centred_square("pre", b, 1)
                for b in range(B):
                    ln_act_rstd(act, S, "pre", b, 1, bank[b][3], sq["pre"][:, b, :])
                for b in range(B):
                    high(b, 1)
                for k in range(1, NE):
                    high_weights(k)
                for b in range(B):
                    rectify(b, 0)
                with act.Fori(0, NIT - 1) as it:
                    n = it + 1
                    experts(it, True)
                    take(0, n)
                    rectify(0, n * NE)
                    take(1, n)
                    for b in range(B):
                        centred_square("post", b, n)
                    rectify(1, n * NE)
                    for b in range(B):
                        ln_act_rstd(act, S, "post", b, n, bank[b][3], sq["post"][:, b, :])
                experts(NIT - 1, False)
                for b in range(B):
                    take(b, NIT)
                for b in range(B):
                    centred_square("post", b, NIT)
                for b in range(B):
                    ln_act_rstd(act, S, "post", b, NIT, bank[b][3], sq["post"][:, b, :])

            @block.gpsimd
            def _(pool):
                for b in range(B):
                    nc.gpsimd.sem_inc(S["done"][b], 1)
                for k in range(NE):
                    e = slice(ORDER[k] * FF, (ORDER[k] + 1) * FF)
                    pool.wait_ge(S["w_hi"][0], k + 1)
                    nc.gpsimd.tensor_tensor(w_lo[:, e], wfc[:, e], w_hi[:, e].bitcast(F32), ALU.subtract).then_inc(S["w_lo"][0], 1)
                with pool.Fori(0, NIT) as it:
                    for b in range(B):
                        pool.wait_ge(S["post_out"][b], it + 1)
                        nc.gpsimd.tensor_tensor(x[:, b, tok(it)], x[:, b, tok(it)], xn["post"][:, b, :], ALU.add).then_inc(S["done"][b], 1)

        release(S)
        experts_scope.close()
        S = sems("gate", ln_names("pre") + " qk kv qv expd plus A la v", NS)
        gated_scope, sbg = scope()
        qs_, ks_, la, vs = (sbg(name, [P, B, N]) for name in ("qs", "ks", "la", "vs"))

        with nc.Block() as block:
            @block.tensor
            def _(pe):
                with pe.Fori(0, PASSES) as it:
                    n = it + 1
                    for t in range(NS):
                        b, cols = group(it, t)
                        ln_pe_center(pe, S, "pre", t, n, x[:, b, cols], two[t][0])
                    for t in range(NS):
                        ln_pe_var(pe, S, "pre", t, n, two[t][1], sq4[t])
                    for t in range(NS):
                        pe.wait_ge(S["pre_out"][t], n)
                        nc.tensor.matmul(two[t][0][:, :], w_g[:, 2 * P:3 * P], xn4[t], start=True, stop=True)
                        for c in range(NC):
                            mm = nc.tensor.matmul(two[t][1][:, c * P:(c + 1) * P], xn4[t][:, c * P:(c + 1) * P],
                                                  w_g[:, 3 * P:4 * P], start=True, stop=True)
                        mm.then_inc(S["kv"][t], 1)
                    for t in range(NS):
                        pe.wait_ge(S["expd"][t], n)
                        nc.tensor.matmul(two[t][0][:, :], w_g[:, 0:P], xn4[t], start=True, stop=True)
                        pe.wait_ge(S["v"][t], n)
                        nc.tensor.matmul(two[t][1][:, :], w_g[:, P:2 * P], xn4[t], start=True, stop=True).then_inc(S["qk"][t], 1)
                    for t in range(NS):
                        pe.wait_ge(S["qv"][t], 2 * n)

            @block.vector
            def _(dve):
                with dve.Fori(0, PASSES) as it:
                    n = it + 1
                    for t in range(NS):
                        ln_dve_scale(dve, S, "pre", t, n, xn4[t], two[t][0], sq4[t])
                    for t in range(NS):
                        b, cols = group(it, t)
                        dve.wait_ge(S["kv"][t], n)
                        dve.wait_ge(S["expd"][t], n)
                        nc.vector.tensor_tensor(chunks(vs[:, b, cols]), chunks(two[t][1][:, :]), over_chunks(b_v), ALU.add
                                                ).then_inc(S["v"][t], 1)
                    for t in range(NS):
                        b, cols = group(it, t)
                        nc.vector.tensor_scalar(cen4[t], cen4[t], 1.0, None, ALU.add).then_inc(S["plus"][t], 1)
                        dve.wait_ge(S["plus"][t], n)
                        nc.vector.reciprocal(la[:, b, cols], cen4[t]).then_inc(S["A"][t], 1)

            @block.scalar
            def _(act):
                nc.scalar.preload_act_table_set(LN_EXP)
                with act.Fori(0, PASSES) as it:
                    n = it + 1
                    for t in range(NS):
                        ln_act_square(act, S, "pre", t, n, two[t][0], sq4[t])
                    for t in range(NS):
                        ln_act_rstd(act, S, "pre", t, n, two[t][1], sq4[t])
                    for t in range(NS):
                        act.wait_ge(S["kv"][t], n)
                        nc.scalar.activation(cen4[t], two[t][0][:, :], ACT.Exp, bias=nb_gate[:, 0:1], scale=-1.0).then_inc(S["expd"][t], 1)
                    for t in range(NS):
                        b, cols = group(it, t)
                        act.wait_ge(S["qk"][t], n)
                        nc.scalar.activation(qs_[:, b, cols], two[t][0][:, :], ACT.Relu, bias=b_g[:, 0:1]).then_inc(S["qv"][t], 1)
                        nc.scalar.activation(ks_[:, b, cols], two[t][1][:, :], ACT.Relu, bias=b_g[:, 1:2]).then_inc(S["qv"][t], 1)
                    for t in range(NS):
                        b, cols = group(it, t)
                        act.wait_ge(S["A"][t], n)
                        nc.scalar.activation(la[:, b, cols], la[:, b, cols], ACT.Ln, bias=eps6[:, :]).then_inc(S["la"][t], 1)

            @block.gpsimd
            def _(pool):
                for t in range(NS):
                    nc.gpsimd.sem_inc(S["pre_in"][t], PASSES)

        release(S)
        S = sems("gla", "eL wk v wkt wktok scores dstate probs nd plus rec init " + ln_names("post") + " done", NS)
        S |= sems("gla", "sum state")
        gla = sbg("gla", [P, 3, NS, G])
        wk, wkt, v3 = ([gla[:, i, t, :] for t in range(NS)] for i in range(3))
        ones = sbg("ones", [P, P])
        st3 = sbg("st3", [P, B, NSLOT, 2 * P])
        pr3 = cen4

        with nc.Block() as block:
            @block.tensor
            def _(pe):
                pe.wait_ge(S["init"][1], 1)
                with pe.Fori(0, PASSES) as it:
                    n = it + 1
                    for t in range(NS):
                        b, first = t % B, (2 * it + t // B) * G
                        pe.wait_ge(S["wk"][t], n)
                        for c in range(NC):
                            mm = nc.tensor.transpose(two[t][0][:, c * P:(c + 1) * P], wk[t][:, c * P:(c + 1) * P], ident[:, :])
                        mm.then_inc(S["wkt"][t], 1)
                        for c in range(NC):
                            mm = nc.tensor.matmul(two[t][1][:, c * P:(c + 1) * P], wk[t][:, c * P:(c + 1) * P],
                                                  qs_[:, b, bass.ds(first + c * P, P)], start=True, stop=True)
                        mm.then_inc(S["scores"][t], 1)
                    for t in range(NS):
                        pe.wait_ge(S["wktok"][t], n)
                        pe.wait_ge(S["probs"][t], n)
                        pe.wait_ge(S["v"][t], n)
                        for c in range(NC):
                            to = c % 2 * 2 * P
                            nc.tensor.matmul(two[t][c // 2][:, to:to + P], wkt[t][:, c * P:(c + 1) * P], v3[t][:, c * P:(c + 1) * P],
                                             start=True, stop=True)
                            mm = nc.tensor.matmul(two[t][c // 2][:, to + P:to + 2 * P], wkt[t][:, c * P:(c + 1) * P], ones[:, :],
                                                  start=True, stop=True)
                        mm.then_inc(S["dstate"][t], 1)
                    for t in range(NS):
                        b, first = t % B, (2 * it + t // B) * G
                        pe.wait_ge(S["state"][b], it * NSLOT + 1 + (t // B + 1) * NC)
                        for half in range(2):
                            for c in range(NC):
                                cs = slice(c * P, (c + 1) * P)
                                nc.tensor.matmul(two[t][half][:, cs], ones[:, :] if half else v3[t][:, cs], pr3[t][:, cs],
                                                 start=True, stop=False)
                                mm = nc.tensor.matmul(two[t][half][:, cs], st3[:, b, t // B * NC + c, half * P:(half + 1) * P],
                                                      qs_[:, b, bass.ds(first + c * P, P)], start=False, stop=True)
                        mm.then_inc(S["nd"][t], 1)
                    for t in range(NS):
                        ln_pe_center(pe, S, "post", t, n, xn4[t], two[t][0])
                    for t in range(NS):
                        ln_pe_var(pe, S, "post", t, n, two[t][1], sq4[t])
                    for t in range(NS):
                        pe.wait_ge(S["post_out"][t], n)

            @block.vector
            def _(dve):
                for b in range(B):
                    back = la[:, b, ::-1]
                    nc.vector.tensor_tensor_scan(back, back, zero[:, 0:1].to_broadcast([P, N]), 0.0, ALU.add, ALU.add
                                                 ).then_inc(S["sum"][b], 1)
                with dve.Fori(0, PASSES) as it:
                    n = it + 1
                    for t in range(NS):
                        b, cols = group(it, t)
                        dve.wait_ge(S["eL"][t], n)
                        nc.vector.tensor_tensor(wk[t], ks_[:, b, cols], cen4[t], ALU.mult).then_inc(S["wk"][t], 1)
                    for t in range(NS):
                        dve.wait_ge(S["scores"][t], n)
                        nc.vector.tensor_tensor(chunks(pr3[t]), chunks(two[t][1][:, :]), over_chunks(causal), ALU.mult
                                                ).then_inc(S["probs"][t], 1)
                    for t in range(NS):
                        b, half = t % B, t // B
                        dve.wait_ge(S["dstate"][t], n)
                        if half == 0:
                            nc.vector.tensor_copy(st3[:, b, 0, :], st3[:, b, NSLOT - 1, :]).then_inc(S["state"][b], 1)
                        for c in range(NC):
                            k = half * NC + c
                            dve.wait_ge(S["state"][b], it * NSLOT + 1 + k)
                            nc.vector.tensor_tensor(st3[:, b, k + 1, :], st3[:, b, k, :],
                                                    two[t][c // 2][:, (c % 2) * 2 * P:(c % 2 + 1) * 2 * P], ALU.add
                                                    ).then_inc(S["state"][b], 1)
                    for t in range(NS):
                        dve.wait_ge(S["plus"][t], n)
                        nc.vector.reciprocal(sq4[t], xn4[t]).then_inc(S["rec"][t], 1)
                        dve.wait_ge(S["rec"][t], n)
                        nc.vector.tensor_tensor(xn4[t], sq4[t], two[t][0][:, :], ALU.mult).then_inc(S["post_in"][t], 1)
                    for t in range(NS):
                        ln_dve_scale(dve, S, "post", t, n, xn4[t], two[t][0], sq4[t])

            @block.scalar
            def _(act):
                nc.scalar.preload_act_table_set(LN_EXP)
                for b in range(B):
                    act.wait_ge(S["sum"][b], 1)
                with act.Fori(0, PASSES) as it:
                    n = it + 1
                    for t in range(NS):
                        b, cols = group(it, t)
                        nc.scalar.activation(cen4[t], la[:, b, cols], ACT.Exp).then_inc(S["eL"][t], 1)
                    for t in range(NS):
                        act.wait_ge(S["wkt"][t], n)
                        nc.scalar.activation(wkt[t], two[t][0][:, :], ACT.Copy).then_inc(S["wktok"][t], 1)
                    for t in range(NS):
                        act.wait_ge(S["nd"][t], n)
                        act.wait_ge(S["done"][t], n)
                        nc.scalar.activation(xn4[t], two[t][1][:, :], ACT.Identity, bias=eps6[:, :]).then_inc(S["plus"][t], 1)
                    for t in range(NS):
                        ln_act_square(act, S, "post", t, n, two[t][0], sq4[t])
                    for t in range(NS):
                        ln_act_rstd(act, S, "post", t, n, two[t][1], sq4[t])

            @block.gpsimd
            def _(pool):
                for b in range(B):
                    nc.gpsimd.memset(st3[:, b, NSLOT - 1, :], 0.0).then_inc(S["init"][0], 1)
                nc.gpsimd.memset(ones[:, :], 1.0).then_inc(S["init"][1], 1)
                for t in range(NS):
                    nc.gpsimd.sem_inc(S["done"][t], 1)
                with pool.Fori(0, PASSES) as it:
                    for t in range(NS):
                        b, cols = group(it, t)
                        nc.gpsimd.tensor_copy(v3[t], vs[:, b, cols]).then_inc(S["v"][t], 1)
                    for t in range(NS):
                        b, cols = group(it, t)
                        pool.wait_ge(S["post_out"][t], it + 1)
                        nc.gpsimd.tensor_tensor(x[:, b, cols], x[:, b, cols], xn4[t], ALU.add).then_inc(S["done"][t], 1)

        release(S)
        gated_scope.close()
        LO, HI = slice(0, DH), slice(DH, P)
        y = [sb(f"stream{i}", [P, B, N + 1]) for i in range(2)]
        qr = sb("qr", [P, B, NM, G])
        kr = sb("kr", [P, B, NM, W + G])
        vt = sb("vt", [P, B, NC, INNER])
        vb = sb("vb", [P, B, NC + 1, INNER])
        y1 = sb("y1", [P, B, G + 1])
        rot = sb("rot", [P, 4, G])
        band = sb("band_bf", [P, NIT, G], BF16)
        prob = [cen["pre"], sq["pre"]]
        probT = [cen["post"], sq["post"]]
        oT = xn["post"]
        gelu = [cen["post"], sq["post"]]
        u = [xn["pre"], xn["post"]]
        VALUE = [0, 3, 0]
        hn = cen["pre"]
        small = sb("small", [P, B, 4, H])

        queries = qr[:, :, :, :].rearrange("p b m g -> p (b m g)")
        raw, band_f32 = queries[:, 0:INPUT], queries[:, INPUT:INPUT + 2 * G]
        hs_hi, hs_lo = (sb(name, [P, B, G], F32R) for name in ("hs_hi", "hs_lo"))

        NU = 2 * B * NC
        S = sems("start", ln_names("pre"), NS)
        with nc.Block() as block:
            @block.sync
            def _(sp):
                sp.dma_start(band_f32, a["band"].rearrange("p k g -> p (k g)")).then_inc(s_band, 16)
                sp.dma_start(raw, a["wi"][0]).then_inc(s_input, 16)
                sp.dma_start(rot[:, :, :], a["rot"][:, :, 0:G]).then_inc(s_rot, 16)

            @block.tensor
            def _(pe):
                with pe.Fori(0, PASSES) as it:
                    n = it + 1
                    for t in range(NS):
                        b, cols = group(it, t)
                        ln_pe_center(pe, S, "pre", t, n, x[:, b, cols], two[t][0])
                    for t in range(NS):
                        ln_pe_var(pe, S, "pre", t, n, two[t][1], sq4[t])
                    for t in range(NS):
                        pe.wait_ge(S["pre_out"][t], 2 * n)

            @block.vector
            def _(dve):
                dve.wait_ge(s_band, 16)
                nc.vector.tensor_copy(band[:, 0, :], band_f32[:, 0:G]).then_inc(s_set, 1)
                for k in range(1, NIT):
                    nc.vector.tensor_copy(band[:, k, :], band_f32[:, G:2 * G]).then_inc(s_set, 1)
                for b in range(B):
                    for l in range(2):
                        nc.vector.memset(y[l][:, b, 0:1], 0.0).then_inc(s_set, 1)
                    nc.vector.memset(vb[:, b, NC, :], 0.0).then_inc(s_set, 1)
                dve.wait_ge(s_set, 6 + NIT + 3 * B)
                with dve.Fori(0, PASSES) as it:
                    n = it + 1
                    for t in range(NS):
                        b, first = t % B, (2 * it + t // B) * G
                        dve.wait_ge(S["pre_rstd"][t], 2 * n)
                        nc.vector.tensor_tensor(y[0][LO, b, bass.ds(first, G)], two[t][0][LO, :], sq4[t][LO, :], ALU.mult
                                                ).then_inc(S["pre_out"][t], 1)
                        nc.vector.tensor_tensor(y[0][HI, b, bass.ds(first + 1, G)], two[t][0][HI, :], sq4[t][HI, :], ALU.mult
                                                ).then_inc(S["pre_out"][t], 1)

            @block.scalar
            def _(act):
                nc.scalar.preload_act_table_set(LN_EXP)
                with act.Fori(0, PASSES) as it:
                    n = it + 1
                    for t in range(NS):
                        ln_act_square(act, S, "pre", t, n, two[t][0], sq4[t])
                    for t in range(NS):
                        ln_act_rstd(act, S, "pre", t, n, two[t][1], sq4[t])

            @block.gpsimd
            def _(pool):
                for t in range(NS):
                    nc.gpsimd.sem_inc(S["pre_in"][t], PASSES)
        release(S)

        for l in range(DEPTH):
            yin, yout = y[l % 2], y[(l + 1) % 2]
            at = [0]

            def part(width, l=l, at=at):
                at[0] += width
                return wl[:, l, at[0] - width:at[0]]

            w_o = part(INNER).rearrange("p (m w) -> p m w", m=NM)
            w_1 = part(2 * HID)
            w_2 = part(3 * P).rearrange("p (m w) -> p m w", m=3)
            PIECE = 4 * P
            PIECES = [0, 4, 1, 2, 3]

            def w_in(first, width):
                return wi_hi[:, first:first + width], wi_lo[:, first:first + width]

            VALUES_AT = {1: (0,), 3: (1,), 6: (2,), 7: (3,)}
            w_v = w_in(2 * 8 * P, INNER)
            S = sems(f"layer{l}", "w_hi w_lo nokeys go hs_hi hs_lo xy sqr nrm r rotd t3 qk halo v vcp sc0 sc1 mx0 mx1 ex0 ex1 rec0 rec1 pn0 pn1 pt0 pt1 ptc0 ptc1 pv oc wo y1 fold hn ag gl u w2 y2 "
                     + ln_names("mid"))
            s_last = [nc.alloc_semaphore(f"s_last{l}{b}") for b in range(B)]
            s_vb = [[nc.alloc_semaphore(f"s_vb{l}{b}{h}") for h in range(2)] for b in range(B)]

            def unit(t):
                return t // 2 % B, t % 2, t // (2 * B)

            with nc.Block() as block:
                @block.sync
                def _(sp):
                    with sp.Fori(0, NIT) as it:
                        n = it + 1
                        for b in range(B):
                            sp.wait_ge(S["vcp"][b], NC * it + 1)
                            sp.dma_start(vb[HI, b, 0, :], vb[HI, b, NC, :]).then_inc(s_last[b], 16)
                        for h in range(2):
                            first, end = h * NC // 2, (h + 1) * NC // 2
                            for b in range(B):
                                sp.wait_ge(S["vcp"][b], NC * it + end)
                                sp.dma_start(vb[LO, b, first:end, :], vt[LO, b, first:end, :]).then_inc(s_vb[b][h], 16)
                                if h == 1:
                                    sp.wait_ge(s_last[b], 16 * n)
                                sp.dma_start(vb[HI, b, first + 1:end + 1, :], vt[HI, b, first:end, :]).then_inc(s_vb[b][h], 16)
                        for b in range(B):
                            sp.wait_ge(S["rotd"][b], 16 * n)
                        sp.dma_start(rot[:, :, :], a["rot"][:, :, bass.ds((n % NIT) * G, G)]).then_inc(s_rot, 16)
                    if l + 1 == DEPTH:
                        sp.wait_ge(s_rot, 16 * (DEPTH * NIT + 1))
                    if l + 1 < DEPTH:
                        for b in range(B):
                            for p in range(2):
                                sp.wait_ge(S[f"sc{p}"][b], NC * NIT)
                        sp.dma_start(raw, a["wi"][l + 1]).then_inc(s_input, 16)

                @block.tensor
                def _(pe):
                    def scores(b, p, c, band_of_chunk):
                        to = bank[b][p]
                        rows = slice(p * DH, (p + 1) * DH)
                        nc.tensor.matmul(to[:, :], ident_bf[:, :], band_of_chunk, start=True, stop=False, skip_group_check=True)
                        for m in range(NM):
                            q0, k0 = c * P, m * P
                            nc.tensor.matmul(to[LO, k0:k0 + W], qr[rows, b, m, q0:q0 + W], kr[rows, b, m, W + q0:2 * W + q0],
                                             start=False, stop=False, skip_group_check=True)
                            nc.tensor.matmul(to[LO, k0 + W:k0 + P], qr[rows, b, m, q0:q0 + W], kr[rows, b, m, q0:W + q0],
                                             start=False, stop=False, skip_group_check=True)
                            mm = nc.tensor.matmul(to[HI, k0:k0 + P], qr[rows, b, m, q0 + W:q0 + P],
                                                  kr[rows, b, m, W + q0:3 * W + q0], start=False, stop=(m == NM - 1),
                                                  skip_group_check=True)
                        mm.then_inc(S[f"sc{p}"][b], 1)

                    def turn(it, b, p, c):
                        pe.wait_ge(S[f"pn{p}"][b], it * NC + c + 1)
                        for m in range(NM):
                            mm = nc.tensor.transpose(bank[b][p][:, m * P:(m + 1) * P], prob[p][:, b, m * P:(m + 1) * P], ident[:, :])
                        mm.then_inc(S[f"pt{p}"][b], 1)

                    def values(it, b, p, c):
                        pe.wait_ge(S[f"ptc{p}"][b], it * NC + c + 1)
                        rows = slice(p * DH, (p + 1) * DH)
                        for m in range(NM):
                            h0 = (2 * m + p) * DH
                            nc.tensor.matmul(bank[b][2][rows, m * P:m * P + W], vb[:, b, c, h0:h0 + DH],
                                             probT[p][:, b, m * P:m * P + W], start=True, stop=True)
                            mm = nc.tensor.matmul(bank[b][2][rows, m * P + W:(m + 1) * P], vt[:, b, c, h0:h0 + DH],
                                                  probT[p][:, b, m * P + W:(m + 1) * P], start=True, stop=True)
                        if p == 1:
                            mm.then_inc(S["pv"][b], 1)

                    def project(it, b, c):
                        pe.wait_ge(S["oc"][b], it * NC + c + 1)
                        for m in range(NM):
                            mm = nc.tensor.matmul(bank[b][3][:, c * P:(c + 1) * P], w_o[:, m, :], oT[:, b, m * P:(m + 1) * P],
                                                  start=(m == 0), stop=(m == NM - 1))
                        mm.then_inc(S["wo"][b], 1)

                    pe.wait_ge(s_layers, 16 * (DEPTH + 2))
                    for j in range(3):
                        for k in range(2):
                            mm = nc.tensor.matmul(bank[0][0][0:HC[j], 3 * k + j:3 * k + j + 1],
                                                  w_1[:, k * HID + j * P:k * HID + j * P + HC[j]], vec[:, l, 5:6],
                                                  start=True, stop=True)
                    mm.then_inc(S["fold"][0], 1)
                    pe.wait_ge(S["fold"][1], 2)
                    with pe.Fori(0, NIT) as it:
                        n = it + 1
                        for m in range(8):
                            if m % 2 == 0:
                                pe.wait_ge(S["w_lo"][0], PIECES.index(m // 2) + 1)
                            for b in range(B):
                                if m:
                                    pe.wait_ge(S["rotd"][b], it * 16 + 2 * m)
                                else:
                                    pe.wait_ge(S["hs_lo"][b], n)
                                h = hs_hi[:, b, :], hs_lo[:, b, :]
                                product(bank[b][0][:, :], *w_in(2 * m * P, P), *h)
                                product(bank[b][1][:, :], *w_in((2 * m + 1) * P, P), *h).then_inc(S["xy"][b], 1)
                            for b in range(B):
                                if m == 0:
                                    pe.wait_ge(S["y2"][b], 2 * it + 1)
                                pe.wait_ge(S["sqr"][b], it * 8 + m + 1)
                                nc.tensor.matmul(bank[b][2][:, :], pair_ones[:, :], sq["pre"][:, b, :], start=True, stop=True
                                                 ).then_inc(S["nrm"][b], 1)
                            for c in VALUES_AT.get(m, ()):
                                pe.wait_ge(S["w_lo"][0], PIECES.index(4) + 1)
                                for b in range(B):
                                    if c:
                                        pe.wait_ge(S["vcp"][b], it * NC + c)
                                    cs = slice(c * P, (c + 1) * P)
                                    product(bank[b][3][:, :], hs_hi[:, b, cs], hs_lo[:, b, cs], *w_v).then_inc(S["v"][b], 1)
                        for t in range(NU + 8):
                            if 0 <= t - 5 < NU:
                                b, p, c = unit(t - 5)
                                if p == 0 and c == 0:
                                    pe.wait_ge(s_last[b], 16 * n)
                                if p == 0 and c % 2 == 0:
                                    pe.wait_ge(s_vb[b][c // 2], 32 * n)
                                    pe.wait_ge(S["vcp"][b], NC * it + c + 2)
                                if p == 0 and c:
                                    pe.wait_ge(S["oc"][b], it * NC + c)
                                values(it, b, p, c)
                            if 0 <= t - 3 < NU:
                                turn(it, *unit(t - 3))
                            if t >= 8 and unit(t - 8)[1] == 1:
                                project(it, unit(t - 8)[0], unit(t - 8)[2])
                            if t < NU:
                                b, p, c = unit(t)
                                if c:
                                    pe.wait_ge(S[f"ptc{p}"][b], it * NC + c)
                                elif p == 0:
                                    pe.wait_ge(S["qk"][b], 8 * n)
                                scores(b, p, c, band[:, 1, :] if c else band[:, it, :])
                        for b in range(B):
                            pe.wait_ge(S["y1"][b], 3 * n)
                            nc.tensor.matmul(bank[b][0][:, :], center_w[:, :], y1[:, b, 0:G], start=True, stop=True
                                             ).then_inc(S["mid_cen"][b], 1)
                        for b in range(B):
                            ln_pe_var(pe, S, "mid", b, n, bank[b][1], sq["pre"][:, b, :])
                        def hidden(j):
                            for b in range(B):
                                if j == 0:
                                    pe.wait_ge(S["hn"][b], n)
                                else:
                                    pe.wait_ge(S["gl"][b], it * 3 + j)
                                if j == 2:
                                    pe.wait_ge(S["u"][b], it * 3 + 1)
                                nc.tensor.matmul(bank[b][VALUE[j]][0:HC[j], :], w_1[:, j * P:j * P + HC[j]], hn[:, b, :],
                                                 start=True, stop=True)
                                nc.tensor.matmul(bank[b][1][0:HC[j], :], w_1[:, HID + j * P:HID + j * P + HC[j]], hn[:, b, :],
                                                 start=True, stop=True).then_inc(S["ag"][b], 1)

                        hidden(0)
                        for j in range(3):
                            if j < 2:
                                hidden(j + 1)
                            for b in range(B):
                                pe.wait_ge(S["u"][b], it * 3 + j + 1)
                                mm = nc.tensor.matmul(bank[b][2][:, :], w_2[0:HC[j], j, :], u[j % 2][0:HC[j], b, :],
                                                      start=(j == 0), stop=(j == 2))
                                mm.then_inc(S["w2"][b], 1)

                @block.vector
                def _(dve):
                    for b in range(B):
                        nc.vector.memset(y1[:, b, G:G + 1], 0.0).then_inc(S["y2"][b], 1)
                        dve.wait_ge(S["y2"][b], 1)
                        nc.vector.memset(kr[:, b, :, G:W + G], 0.0).then_inc(S["nokeys"][b], 1)
                    def rest(b, n, group):
                        dve.wait_ge(S["hs_hi"][b], n)
                        nc.vector.tensor_tensor(hs_lo[:, b, :], yin[:, b, group], hs_hi[:, b, :].bitcast(F32), ALU.subtract
                                                ).then_inc(S["hs_lo"][b], 1)

                    for b in range(B):
                        rest(b, 1, slice(0, G))
                    dve.wait_ge(S["fold"][0], 1)
                    biases = vec[:, l, 6:12].rearrange("p (k j) -> p k j", k=2)
                    folded = bank[0][0][:, 0:6].rearrange("p (k j) -> p k j", k=2)
                    for rows, cols in ((slice(0, P), slice(0, 2)), (slice(0, HC[2]), slice(2, 3))):
                        nc.vector.tensor_tensor(biases[rows, :, cols], biases[rows, :, cols], folded[rows, :, cols], ALU.add
                                                ).then_inc(S["fold"][1], 1)
                    for k, piece in enumerate(PIECES):
                        cs = slice(piece * PIECE, (piece + 1) * PIECE)
                        dve.wait_ge(S["w_hi"][0], k + 1)
                        nc.vector.tensor_tensor(wi_lo[:, cs], raw[:, cs], wi_hi[:, cs].bitcast(F32), ALU.subtract
                                                ).then_inc(S["w_lo"][0], 1)
                    dve.wait_ge(S["w_lo"][0], len(PIECES))
                    with dve.Fori(0, NIT) as it:
                        n = it + 1
                        dve.wait_ge(s_rot, 16 * (l * NIT + n))
                        for m in range(8):
                            s0, t0 = (0, 0) if m < NM else (2, 2)
                            for b in range(B):
                                dve.wait_ge(S["xy"][b], it * 8 + m + 1)
                                if m:
                                    dve.wait_ge(S["qk"][b], it * 8 + m)
                                nc.vector.scalar_tensor_tensor(xn["pre"][:, b, :], bank[b][1][:, :], vec[:, l, s0 + 1:s0 + 2],
                                                               rot[:, t0 + 1, :], ALU.mult, ALU.mult).then_inc(S["rotd"][b], 1)
                                dve.wait_ge(S["sqr"][b], it * 8 + m + 1)
                                nc.vector.scalar_tensor_tensor(cen["pre"][:, b, :], bank[b][0][:, :], vec[:, l, s0:s0 + 1],
                                                               rot[:, t0, :], ALU.mult, ALU.mult).then_inc(S["rotd"][b], 1)
                            for b in range(B):
                                dve.wait_ge(S["t3"][b], it * 8 + m + 1)
                                dve.wait_ge(S["r"][b], (it * 8 + m + 1) * 2)
                                if m == NM:
                                    dve.wait_ge(S["halo"][b], n)
                                to = qr[:, b, m, :] if m < NM else kr[:, b, m - NM, W:W + G]
                                nc.vector.scalar_tensor_tensor(to, cen["post"][:, b, :], 1e12, cen["pre"][:, b, :], ALU.min, ALU.mult
                                                               ).then_inc(S["qk"][b], 1)
                        for t in range(NU + 1):
                            if t < NU:
                                b, p, c = unit(t)
                                hs4 = slice(p * NM, (p + 1) * NM)
                                dve.wait_ge(S[f"sc{p}"][b], it * NC + c + 1)
                                nc.vector.tensor_reduce(small[:, b, 3, hs4], bank[b][p][:, :].rearrange("p (m k) -> p m k", m=NM),
                                                        AX, ALU.max).then_inc(S[f"mx{p}"][b], 1)
                                dve.wait_ge(S[f"mx{p}"][b], (it * NC + c) * 2 + 1)
                                nc.vector.tensor_scalar(small[:, b, 0, hs4], small[:, b, 3, hs4], -8.0, None, ALU.mult
                                                        ).then_inc(S[f"mx{p}"][b], 1)
                            if t:
                                b, p, c = unit(t - 1)
                                hs4 = slice(p * NM, (p + 1) * NM)
                                dve.wait_ge(S[f"ex{p}"][b], it * NC + c + 1)
                                nc.vector.reciprocal(small[:, b, 2, hs4], small[:, b, 1, hs4]).then_inc(S[f"rec{p}"][b], 1)
                                dve.wait_ge(S[f"rec{p}"][b], it * NC + c + 1)
                                v = prob[p][:, b, :].rearrange("p (m k) -> p m k", m=NM)
                                nc.vector.tensor_tensor(v, v, small[:, b, 2, hs4][:, :, None].to_broadcast([P, NM, P]), ALU.mult
                                                        ).then_inc(S[f"pn{p}"][b], 1)
                        for b in range(B):
                            dve.wait_ge(S["wo"][b], NC * n)
                            nc.vector.tensor_copy(y1[HI, b, 0:1], y1[HI, b, G:G + 1]).then_inc(S["y1"][b], 1)
                            dve.wait_ge(S["y1"][b], 3 * it + 1)
                            nc.vector.tensor_tensor(y1[LO, b, 0:G], yin[LO, b, bass.ds(it * G, G)], bank[b][3][LO, :], ALU.add
                                                    ).then_inc(S["y1"][b], 1)
                            nc.vector.tensor_tensor(y1[HI, b, 1:G + 1], yin[HI, b, bass.ds(it * G + 1, G)], bank[b][3][HI, :], ALU.add
                                                    ).then_inc(S["y1"][b], 1)
                            dve.wait_ge(S["y1"][b], 3 * n)
                        for b in range(B):
                            rest(b, n + 1, bass.ds((n % NIT) * G, G))
                        for b in range(B):
                            dve.wait_ge(S["mid_rstd"][b], 2 * n)
                            nc.vector.scalar_tensor_tensor(hn[:, b, :], bank[b][0][:, :], vec[:, l, 4:5], sq["pre"][:, b, :],
                                                           ALU.mult, ALU.mult).then_inc(S["hn"][b], 1)
                        for j in range(3):
                            for b in range(B):
                                rows = slice(0, HC[j])
                                dve.wait_ge(S["gl"][b], it * 3 + j + 1)
                                if j == 2:
                                    dve.wait_ge(S["w2"][b], it * 3 + 1)
                                nc.vector.scalar_tensor_tensor(u[j % 2][rows, b, :], bank[b][VALUE[j]][rows, :],
                                                               vec[rows, l, 6 + j:7 + j], gelu[j % 2][rows, b, :],
                                                               ALU.add, ALU.mult).then_inc(S["u"][b], 1)
                        for b in range(B):
                            dve.wait_ge(S["w2"][b], 3 * n)
                            nc.vector.scalar_tensor_tensor(yout[LO, b, bass.ds(it * G, G)], bank[b][2][LO, :], vec[LO, l, 12:13],
                                                           y1[LO, b, 0:G], ALU.add, ALU.add).then_inc(S["y2"][b], 1)
                            nc.vector.scalar_tensor_tensor(yout[HI, b, bass.ds(it * G + 1, G)], bank[b][2][HI, :], vec[HI, l, 12:13],
                                                           y1[HI, b, 1:G + 1], ALU.add, ALU.add).then_inc(S["y2"][b], 1)
                            dve.wait_ge(S["y2"][b], 2 * n + 1)

                @block.scalar
                def _(act):
                    nc.scalar.preload_act_table_set(LN_EXP)
                    def high(b, group):
                        nc.scalar.activation(hs_hi[:, b, :], yin[:, b, group], ACT.Copy).then_inc(S["hs_hi"][b], 1)

                    for b in range(B):
                        high(b, slice(0, G))
                    act.wait_ge(s_input, 16 * (l + 1))
                    for piece in PIECES:
                        cs = slice(piece * PIECE, (piece + 1) * PIECE)
                        nc.scalar.activation(wi_hi[:, cs], raw[:, cs], ACT.Copy).then_inc(S["w_hi"][0], 1)
                    with act.Fori(0, NIT) as it:
                        n = it + 1
                        for m in range(8):
                            for b in range(B):
                                act.wait_ge(S["xy"][b], it * 8 + m + 1)
                                nc.scalar.activation(sq["pre"][:, b, :], bank[b][0][:, :], ACT.Square).then_inc(S["sqr"][b], 1)
                            for b in range(B):
                                act.wait_ge(S["nrm"][b], it * 8 + m + 1)
                                if m:
                                    act.wait_ge(S["qk"][b], it * 8 + m)
                                nc.scalar.activation(cen["post"][:, b, :], bank[b][2][:, :], ACT.Ln, scale=2.0 ** 20).then_inc(S["r"][b], 1)
                                act.wait_ge(S["r"][b], (it * 8 + m) * 2 + 1)
                                nc.scalar.activation(cen["post"][:, b, :], cen["post"][:, b, :], ACT.Exp, scale=-0.5, bias=ten_ln2[:, :]
                                                     ).then_inc(S["r"][b], 1)
                            for c in VALUES_AT.get(m, ()):
                                for b in range(B):
                                    act.wait_ge(S["v"][b], it * NC + c + 1)
                                    nc.scalar.activation(vt[:, b, c, :], bank[b][3][:, :], ACT.Copy).then_inc(S["vcp"][b], 1)
                        for t in range(NU + 5):
                            if t >= 5 and unit(t - 5)[1] == 1:
                                b, p, c = unit(t - 5)
                                act.wait_ge(S["pv"][b], it * NC + c + 1)
                                nc.scalar.activation(oT[:, b, :], bank[b][2][:, :], ACT.Copy).then_inc(S["oc"][b], 1)
                            if 0 <= t - 2 < NU:
                                b, p, c = unit(t - 2)
                                act.wait_ge(S[f"pt{p}"][b], it * NC + c + 1)
                                nc.scalar.activation(probT[p][:, b, :], bank[b][p][:, :], ACT.Copy).then_inc(S[f"ptc{p}"][b], 1)
                            if t < NU:
                                b, p, c = unit(t)
                                act.wait_ge(S[f"mx{p}"][b], (it * NC + c + 1) * 2)
                                for m in range(NM):
                                    k = p * NM + m
                                    ex = nc.scalar.activation(prob[p][:, b, m * P:(m + 1) * P], bank[b][p][:, m * P:(m + 1) * P],
                                                              ACT.Exp, bias=small[:, b, 0, k:k + 1], scale=8.0,
                                                              accum_out=small[:, b, 1, k:k + 1])
                                ex.then_inc(S[f"ex{p}"][b], 1)
                        for b in range(B):
                            high(b, bass.ds((n % NIT) * G, G))
                        for b in range(B):
                            ln_act_square(act, S, "mid", b, n, bank[b][0], sq["pre"][:, b, :])
                        for b in range(B):
                            ln_act_rstd(act, S, "mid", b, n, bank[b][1], sq["pre"][:, b, :])
                        nc.scalar.preload_act_table_set("gelu_and_others")
                        for j in range(3):
                            for b in range(B):
                                rows = slice(0, HC[j])
                                act.wait_ge(S["ag"][b], it * 3 + j + 1)
                                if j == 2:
                                    act.wait_ge(S["u"][b], it * 3 + 1)
                                nc.scalar.activation(gelu[j % 2][rows, b, :], bank[b][1][rows, :], ACT.Gelu, bias=vec[rows, l, 9 + j:10 + j]
                                                     ).then_inc(S["gl"][b], 1)
                        nc.scalar.preload_act_table_set(LN_EXP)

                @block.gpsimd
                def _(pool):
                    for b in range(B):
                        pool.wait_ge(S["nokeys"][b], 1)
                    with pool.Fori(0, NIT) as it:
                        n = it + 1
                        for b in range(B):
                            pool.wait_ge(S["xy"][b], it * 8 + 1)
                            nc.gpsimd.sem_inc(S["go"][b], 1)
                            nc.gpsimd.tensor_copy(kr[:, b, :, 0:W], kr[:, b, :, G:W + G]).then_inc(S["halo"][b], 1)
                        for m in range(8):
                            for b in range(B):
                                pool.wait_ge(S["rotd"][b], (it * 8 + m + 1) * 2)
                                nc.gpsimd.tensor_tensor(cen["pre"][:, b, :], cen["pre"][:, b, :], xn["pre"][:, b, :], ALU.add
                                                        ).then_inc(S["t3"][b], 1)
            release(S)

        S = sems("end", ln_names("post") + " half done", NS)
        yf = y[DEPTH % 2]
        s_out = sem("s_out")
        with nc.Block() as block:
            @block.sync
            def _(sp):
                for i in range(PASSES):
                    for t in range(NS):
                        first = (2 * i + t // B) * G
                        sp.wait_ge(S["done"][t], i + 2)
                        sp.dma_start(out[:, t % B * N + first:t % B * N + first + G], x[:, t % B, first:first + G]).then_inc(s_out, 16)
                sp.wait_ge(s_out, 16 * NS * PASSES)

            @block.tensor
            def _(pe):
                with pe.Fori(0, PASSES) as it:
                    n = it + 1
                    for t in range(NS):
                        ln_pe_center(pe, S, "post", t, n, cen4[t], two[t][0])
                    for t in range(NS):
                        ln_pe_var(pe, S, "post", t, n, two[t][1], sq4[t])

            @block.vector
            def _(dve):
                with dve.Fori(0, PASSES) as it:
                    n = it + 1
                    for t in range(NS):
                        ln_dve_scale(dve, S, "post", t, n, xn4[t], two[t][0], sq4[t])

            @block.scalar
            def _(act):
                with act.Fori(0, PASSES) as it:
                    n = it + 1
                    for t in range(NS):
                        b, first = t % B, (2 * it + t // B) * G
                        act.wait_ge(S["done"][t], n)
                        nc.scalar.activation(cen4[t][LO, :], yf[LO, b, bass.ds(first, G)], ACT.Copy).then_inc(S["half"][t], 1)
                        nc.scalar.activation(cen4[t][HI, :], yf[HI, b, bass.ds(first + 1, G)], ACT.Copy).then_inc(S["post_in"][t], 1)
                    for t in range(NS):
                        ln_act_square(act, S, "post", t, n, two[t][0], sq4[t])
                    for t in range(NS):
                        ln_act_rstd(act, S, "post", t, n, two[t][1], sq4[t])

            @block.gpsimd
            def _(pool):
                for t in range(NS):
                    nc.gpsimd.sem_inc(S["done"][t], 1)
                with pool.Fori(0, PASSES) as it:
                    for t in range(NS):
                        b, cols = group(it, t)
                        pool.wait_ge(S["post_out"][t], it + 1)
                        nc.gpsimd.tensor_tensor(x[:, b, cols], x[:, b, cols], xn4[t], ALU.add).then_inc(S["done"][t], 1)



def kernel(**inputs):
    import concourse.bacc as bacc
    from concourse.bass_utils import run_bass_kernel_spmd

    f = {k: np.asarray(v) for k, v in inputs.items()}
    arrays = dict(constants())
    arrays["xT"] = f["L0_attn_x"].reshape(B * N, P).T
    arrays["wqkvT"] = f["L0_attn_W_qkv"].T
    bq = f["L0_attn_b_qkv"]
    arrays["b_qkT"] = bq[:2 * P].reshape(2, P).T
    arrays["b_kv"] = bq[None, P:]
    arrays["w_gT"] = np.concatenate([f[f"L1_attn_W_{n}"].T for n in "qkav"], 1)
    arrays["b_gT"] = np.stack([f[f"L1_attn_b_{n}"] for n in "qka"], 1)
    arrays["b_v"] = f["L1_attn_b_v"][None, :]
    wl, wi = [], []
    order = np.arange(2 * INNER).reshape(-1, 2, DH // 2)[:, ::-1].reshape(-1)
    for l in range(DEPTH):
        w, wo, w2 = f["L1_ffn_wqkv"][l], f["L1_ffn_wo"][l], f["L1_ffn_w2"][l]
        w2 = np.concatenate([w2, np.zeros((3 * P - HID, P), w2.dtype)], 0)
        pairs = np.stack([w[:, :2 * INNER].reshape(P, 8, P), w[:, order].reshape(P, 8, P)], 2)
        wi.append(np.concatenate([pairs.reshape(P, -1), w[:, 2 * INNER:]], 1))
        wl.append(np.concatenate([wo.reshape(NM, P, P).transpose(1, 0, 2).reshape(P, -1), f["L1_ffn_w1"][l],
                                  w2.reshape(3, P, P).transpose(1, 0, 2).reshape(P, -1)], 1))
    arrays["wl"], arrays["wi"] = np.stack(wl), np.stack(wi)
    vec = np.zeros((P, DEPTH, 13), np.float32)
    for l in range(DEPTH):
        for i, n in enumerate(("q", "k")):
            s = f[f"L1_ffn_{n}_scale"][l]
            vec[:, l, 2 * i] = np.concatenate([s, s])
            s = np.concatenate([s[DH // 2:], s[:DH // 2]])
            vec[:, l, 2 * i + 1] = np.concatenate([s, s])
        vec[:, l, 4] = f["L1_ffn_ln_g"][l]
        vec[:, l, 5] = f["L1_ffn_ln_b"][l]
        for j in range(3):
            vec[:HC[j], l, 6 + j] = f["L1_ffn_b1"][l, j * P:j * P + HC[j]]
            vec[:HC[j], l, 9 + j] = f["L1_ffn_b1"][l, HID + j * P:HID + j * P + HC[j]]
        vec[:, l, 12] = f["L1_ffn_b2"][l]
    arrays["vec"] = vec
    arrays["routerT"] = f["L0_ffn_router_w"].T
    fc = np.concatenate([f["L0_ffn_w_fc"], f["L0_ffn_shared_fc"][None]], 0)
    pj = np.concatenate([f["L0_ffn_w_proj"], f["L0_ffn_shared_proj"][None]], 0)
    arrays["wfcT"] = fc.reshape(NE * FF, P).T
    arrays["wpjT"] = pj.reshape(NE, P, NF, P).transpose(3, 0, 2, 1)

    nc = bacc.Bacc("TRN2", target_bir_lowering=False, num_devices=1)
    arrays = {k: np.ascontiguousarray(v) for k, v in arrays.items()}
    aps = {k: nc.dram_tensor(f"in_{k}", v.shape, mybir.dt.from_np(v.dtype), kind="ExternalInput").ap() for k, v in arrays.items()}
    out = nc.dram_tensor("out_T", (P, B * N), F32, kind="ExternalOutput").ap()
    sandwich_kernel(nc, aps, out)
    r = run_bass_kernel_spmd(nc, [{f"in_{k}": v for k, v in arrays.items()}], core_ids=[0])
    return np.ascontiguousarray(r.results[0]["out_T"].T).reshape(B, N, P)
```
